# Optimizing a Trainium2 kernel written in Bass

```python
import numpy as np
import jax
import jax.numpy as jnp

def _softmax(x, axis=-1):
    return jax.nn.softmax(x, axis=axis)

def _gelu(x):
    return jax.nn.gelu(x, approximate=True)

def _silu(x):
    return jax.nn.silu(x)

def _sigmoid(x):
    return jax.nn.sigmoid(x)

def _layernorm(x, axis=-1, eps=1e-05):
    m = jnp.mean(x, axis=axis, keepdims=True)
    v = jnp.var(x, axis=axis, keepdims=True)
    return (x - m) / jnp.sqrt(v + eps)

def _scatter_add(tgt, idx, src, axis=0):
    return tgt.at[idx].add(src)

def _segment_sum(src, seg, n):
    return jax.ops.segment_sum(src, seg, n)
kernel_name = 'mk_seq_preln_d1_jaxref_r8_d64e5b'

def setup_inputs(seed: int=0):
    np.random.seed(seed)
    _w = jnp.asarray

    def _L0_attn_setup():
        import jax, jax.numpy as jnp
        import numpy as np
        D_MODEL = 256
        EXPAND = 2
        HEADDIM = 64
        D_STATE = 128
        D_CONV = 4
        NGROUPS = 1
        CHUNK = 32
        EPS = 1e-05
        D_INNER = EXPAND * D_MODEL
        NHEADS = D_INNER // HEADDIM
        CONV_DIM = D_INNER + 2 * NGROUPS * D_STATE
        D_IN_PROJ = 2 * D_INNER + 2 * NGROUPS * D_STATE + NHEADS
        BATCH, SEQLEN = (2, 256)

        def segsum(a):
            T = a.shape[-1]
            cs = jnp.cumsum(a, axis=-1)
            d = cs[..., :, None] - cs[..., None, :]
            mask = jnp.tril(jnp.ones((T, T), dtype=bool))
            return jnp.where(mask, d, -jnp.inf)
        key = jax.random.key(seed)
        ks = jax.random.split(key, 8)
        u = jax.random.normal(ks[0], (BATCH, SEQLEN, D_MODEL), jnp.float32)
        in_proj_w = jax.random.normal(ks[1], (D_IN_PROJ, D_MODEL), jnp.float32) / np.sqrt(D_MODEL).astype(np.float32)
        conv_w = jax.random.normal(ks[2], (CONV_DIM, D_CONV), jnp.float32) / np.sqrt(D_CONV).astype(np.float32)
        conv_b = jnp.zeros((CONV_DIM,), jnp.float32)
        dt0 = jnp.exp(jax.random.uniform(ks[3], (NHEADS,), jnp.float32) * (np.log(0.1) - np.log(0.001)) + np.log(0.001))
        dt0 = jnp.clip(dt0, 0.0001, None)
        dt_bias = dt0 + jnp.log(-jnp.expm1(-dt0))
        A_log = jnp.log(jax.random.uniform(ks[4], (NHEADS,), jnp.float32, minval=1.0, maxval=16.0))
        D = jnp.ones((NHEADS,), jnp.float32)
        norm_w = jnp.ones((D_INNER,), jnp.float32)
        out_proj_w = jax.random.normal(ks[5], (D_MODEL, D_INNER), jnp.float32) / np.sqrt(D_INNER).astype(np.float32)
        return dict(u=u, in_proj_w=in_proj_w, conv_w=conv_w, conv_b=conv_b, dt_bias=dt_bias, A_log=A_log, D=D, norm_w=norm_w, out_proj_w=out_proj_w)
    _L0_attn_in = _L0_attn_setup()

    def _L0_ffn_setup():
        import jax, jax.numpy as jnp
        import numpy as np
        D = 256
        F = 176
        E = 8
        TOPK = 2
        N_SHARED = 2
        ROUTE_SCALE = 1.0

        def _swiglu(x, w1, w2, w3):
            return jax.nn.silu(x @ w1) * (x @ w3) @ w2
        key = jax.random.key(seed)
        ks = jax.random.split(key, 8)
        s = 0.02
        x = jax.random.normal(ks[0], (2, 128, D), dtype=jnp.float32)
        gate_w = jax.random.normal(ks[1], (D, E), dtype=jnp.float32) * s
        Fs = F * N_SHARED
        sw1 = jax.random.normal(ks[2], (D, Fs), dtype=jnp.float32) * s
        sw2 = jax.random.normal(ks[3], (Fs, D), dtype=jnp.float32) * s
        sw3 = jax.random.normal(ks[4], (D, Fs), dtype=jnp.float32) * s
        rw1 = jax.random.normal(ks[5], (E, D, F), dtype=jnp.float32) * s
        rw2 = jax.random.normal(ks[6], (E, F, D), dtype=jnp.float32) * s
        rw3 = jax.random.normal(ks[7], (E, D, F), dtype=jnp.float32) * s
        return {'x': x, 'gate_w': gate_w, 'sw1': sw1, 'sw2': sw2, 'sw3': sw3, 'rw1': rw1, 'rw2': rw2, 'rw3': rw3}
    _L0_ffn_in = _L0_ffn_setup()
    _d = {'L0_attn_u': _L0_attn_in['u'], 'L0_attn_in_proj_w': _L0_attn_in['in_proj_w'], 'L0_attn_conv_w': _L0_attn_in['conv_w'], 'L0_attn_conv_b': _L0_attn_in['conv_b'], 'L0_attn_dt_bias': _L0_attn_in['dt_bias'], 'L0_attn_A_log': _L0_attn_in['A_log'], 'L0_attn_D': _L0_attn_in['D'], 'L0_attn_norm_w': _L0_attn_in['norm_w'], 'L0_attn_out_proj_w': _L0_attn_in['out_proj_w'], 'L0_ffn_gate_w': _L0_ffn_in['gate_w'], 'L0_ffn_sw1': _L0_ffn_in['sw1'], 'L0_ffn_sw2': _L0_ffn_in['sw2'], 'L0_ffn_sw3': _L0_ffn_in['sw3'], 'L0_ffn_rw1': _L0_ffn_in['rw1'], 'L0_ffn_rw2': _L0_ffn_in['rw2'], 'L0_ffn_rw3': _L0_ffn_in['rw3']}
    _x0 = _d['L0_attn_u']
    _d['L0_attn_u'] = jax.random.normal(jax.random.fold_in(jax.random.key(seed), 1), (4, 1024, 256), dtype=_x0.dtype)
    del _x0
    return _d

def reference(L0_attn_u, L0_attn_in_proj_w, L0_attn_conv_w, L0_attn_conv_b, L0_attn_dt_bias, L0_attn_A_log, L0_attn_D, L0_attn_norm_w, L0_attn_out_proj_w, L0_ffn_gate_w, L0_ffn_sw1, L0_ffn_sw2, L0_ffn_sw3, L0_ffn_rw1, L0_ffn_rw2, L0_ffn_rw3):

    def _L0_attn_ref(u, in_proj_w, conv_w, conv_b, dt_bias, A_log, D, norm_w, out_proj_w):
        import jax, jax.numpy as jnp
        import numpy as np
        D_MODEL = 256
        EXPAND = 2
        HEADDIM = 64
        D_STATE = 128
        D_CONV = 4
        NGROUPS = 1
        CHUNK = 32
        EPS = 1e-05
        D_INNER = EXPAND * D_MODEL
        NHEADS = D_INNER // HEADDIM
        CONV_DIM = D_INNER + 2 * NGROUPS * D_STATE
        D_IN_PROJ = 2 * D_INNER + 2 * NGROUPS * D_STATE + NHEADS
        BATCH, SEQLEN = (2, 256)

        def segsum(a):
            T = a.shape[-1]
            cs = jnp.cumsum(a, axis=-1)
            d = cs[..., :, None] - cs[..., None, :]
            mask = jnp.tril(jnp.ones((T, T), dtype=bool))
            return jnp.where(mask, d, -jnp.inf)
        b, l, _ = u.shape
        zxbcdt = jnp.einsum('bld,ed->ble', u, in_proj_w)
        z = zxbcdt[..., :D_INNER]
        xBC = zxbcdt[..., D_INNER:D_INNER + CONV_DIM]
        dt = zxbcdt[..., D_INNER + CONV_DIM:]
        xp = jnp.pad(xBC, ((0, 0), (D_CONV - 1, 0), (0, 0)))
        conv = conv_b
        for k in range(D_CONV):
            conv = conv + xp[:, k:k + l, :] * conv_w[:, k]
        xBC = jax.nn.silu(conv)
        x = xBC[..., :D_INNER]
        Bm = xBC[..., D_INNER:D_INNER + D_STATE]
        Cm = xBC[..., D_INNER + D_STATE:]
        dtv = jax.nn.softplus(dt + dt_bias)
        A = -jnp.exp(A_log)
        xh = x.reshape(b, l, NHEADS, HEADDIM)
        c = l // CHUNK
        xc = (xh * dtv[..., None]).reshape(b, c, CHUNK, NHEADS, HEADDIM)
        Ac = (dtv * A).reshape(b, c, CHUNK, NHEADS).transpose(0, 3, 1, 2)
        Bc = Bm.reshape(b, c, CHUNK, D_STATE)
        Cc = Cm.reshape(b, c, CHUNK, D_STATE)
        Acum = jnp.cumsum(Ac, axis=-1)
        Lmat = jnp.exp(segsum(Ac))
        Y_diag = jnp.einsum('bcqn,bcsn,bhcqs,bcshp->bcqhp', Cc, Bc, Lmat, xc)
        decay_states = jnp.exp(Acum[..., -1:] - Acum)
        states = jnp.einsum('bcsn,bhcs,bcshp->bchpn', Bc, decay_states, xc)
        chunk_decay = jnp.exp(Acum[..., -1])

        def step(S, inp):
            st, dec = inp
            return (dec[..., None, None] * S + st, S)
        S0 = jnp.zeros((b, NHEADS, HEADDIM, D_STATE), xc.dtype)
        _, prev = jax.lax.scan(step, S0, (states.transpose(1, 0, 2, 3, 4), chunk_decay.transpose(2, 0, 1)))
        prev = prev.transpose(1, 0, 2, 3, 4)
        Y_off = jnp.einsum('bcqn,bchpn,bhcq->bcqhp', Cc, prev, jnp.exp(Acum))
        y = (Y_diag + Y_off).reshape(b, l, NHEADS, HEADDIM)
        y = y + D[:, None] * xh
        y = y.reshape(b, l, D_INNER) * jax.nn.silu(z)
        y = y * jax.lax.rsqrt(jnp.mean(jnp.square(y), axis=-1, keepdims=True) + EPS) * norm_w
        return jnp.einsum('bld,ed->ble', y, out_proj_w)

    def _L0_ffn_ref(x, gate_w, sw1, sw2, sw3, rw1, rw2, rw3):
        import jax, jax.numpy as jnp
        import numpy as np
        D = 256
        F = 176
        E = 8
        TOPK = 2
        N_SHARED = 2
        ROUTE_SCALE = 1.0

        def _swiglu(x, w1, w2, w3):
            return jax.nn.silu(x @ w1) * (x @ w3) @ w2
        B, T, _ = x.shape
        xf = x.reshape(-1, D)
        N = xf.shape[0]
        y = _swiglu(xf, sw1, sw2, sw3)
        scores = jax.nn.softmax(xf @ gate_w, axis=-1)
        weights, indices = jax.lax.top_k(scores, TOPK)
        weights = weights * ROUTE_SCALE
        cw = jnp.zeros((N, E), dtype=xf.dtype).at[jnp.arange(N)[:, None], indices].add(weights)
        for e in range(E):
            h = _swiglu(xf, rw1[e], rw2[e], rw3[e])
            y = y + cw[:, e:e + 1] * h
        return y.reshape(B, T, D)
    x = L0_attn_u
    x = x + _L0_attn_ref(_layernorm(x, axis=-1), L0_attn_in_proj_w, L0_attn_conv_w, L0_attn_conv_b, L0_attn_dt_bias, L0_attn_A_log, L0_attn_D, L0_attn_norm_w, L0_attn_out_proj_w)
    x = x + _L0_ffn_ref(_layernorm(x, axis=-1), L0_ffn_gate_w, L0_ffn_sw1, L0_ffn_sw2, L0_ffn_sw3, L0_ffn_rw1, L0_ffn_rw2, L0_ffn_rw3)
    return x

_drawn_inputs = setup_inputs


def setup_inputs(seed=0):
    import zlib

    import numpy as np

    out = dict(_drawn_inputs(seed))
    spreads = {'L0_attn_conv_b': (0.0, 0.1), 'L0_attn_D': (1.0, 0.2), 'L0_attn_norm_w': (1.0, 0.2)}
    factors = {'L0_ffn_gate_w': 8.0,
     'L0_ffn_sw1': 4.123,
     'L0_ffn_sw2': 4.069,
     'L0_ffn_sw3': 4.063,
     'L0_ffn_rw1': 8.0,
     'L0_ffn_rw2': 8.0,
     'L0_ffn_rw3': 8.0}
    for name, (base, spread) in spreads.items():
        noise = np.random.default_rng([zlib.crc32(name.encode()), seed]).standard_normal(out[name].shape)
        drawn = base * np.exp(spread * noise) if base else spread * noise
        out[name] = jnp.asarray(drawn.astype(out[name].dtype))
    for name, factor in factors.items():
        out[name] = (out[name] * factor).astype(out[name].dtype)
    return out
```

```python
from contextlib import ExitStack

import concourse.bass as bass
from concourse import mybir

F32 = mybir.dt.float32
F32R = mybir.dt.float32r
ALU = mybir.AluOpType
ACT = mybir.ActivationFunctionType
AX = mybir.AxisListType

P = 128
DM = 256
KD = DM // P
DI = 512
H = 8
HD = DI // H
NST = 128
TAPS = 4
XBC = DI + 2 * NST
NB = XBC // P
IB, IC = 4, 5
ZH = (H + DI) // 2
ZD = 2 * ZH
WIN = ZD + XBC
KI = DI // P
TOK = 512
CH = TOK // P
SEQ = 2
EPS = 1e-5
E = 8
FE = 176
FS = 352
SB = -(-FS // P)
GROW = FS - (SB - 1) * P
RB = E * FE // P
FB = SB + RB
GROUPS = [(0, 3), (3, 7), (7, 11), (11, FB)]
V_TAP = 0
V_BIAS = V_TAP + NB * TAPS
V_NORM = V_BIAS + NB
V_DT = V_NORM + KI
V_A = V_DT + H
V_D = V_A + H
V_ALL = V_D + H


class Count:

    def __init__(self, handle, per, ahead):
        self.handle, self.per, self.ahead = handle, per, ahead


def need(eng, count, s, k):
    value = count.per * (s + 1 if count.ahead else s) + k
    if isinstance(value, int) and value <= 0:
        return
    eng.wait_ge(count.handle, value)


def need_alone(eng, count, s, k, carrier):
    need(eng, count, s, k)
    if not isinstance(s, int):
        eng.sem_inc(carrier.handle, 1)


def sig(ins, count):
    ins.then_inc(count.handle, 1)


def credit(eng, *counts):
    for c in counts:
        assert c.ahead
        eng.sem_inc(c.handle, c.per)


def product(nc, out, lh, ll, rh, rl, first, last):
    nc.tensor.matmul(out, ll, rh, start=first, stop=False)
    nc.tensor.matmul(out, lh, rl, start=False, stop=False)
    return nc.tensor.matmul(out, lh, rh, start=False, stop=last)


def flat(ap):
    return ap.rearrange("p a b -> p (a b)")


def mixer(nc, NS, u_v, win, wo, vec, x1_d):
    ctx = ExitStack()
    with ctx:
        def sb(name, shape, dt=F32):
            return ctx.enter_context(nc.sbuf_tensor(name, shape, dt))

        def sem(name, per=1, ahead=False):
            return Count(ctx.enter_context(nc.semaphore(name)), per, ahead)

        ident = sb("ident", [P, P])
        win_h = sb("win_h", [P, KD, WIN], F32R)
        win_l = sb("win_l", [P, KD, WIN], F32R)
        wo_h = sb("wo_h", [P, KI, DM], F32R)
        wo_l = sb("wo_l", [P, KI, DM], F32R)
        vecs = sb("vecs", [P, V_ALL])
        causal = sb("causal", [P, P])
        after_f = sb("after_f", [P, P])
        after = sb("after", [P, P], F32R)
        ones = sb("ones", [P, P])
        neg_half = sb("neg_half", [P, CH])
        exp_a = sb("exp_a", [P, H])
        u_ln = sb("u_ln", [P, CH, DM])
        bst = sb("bst", [P, CH, 6])
        mv = sb("mv", [P, CH, 2])
        ve = sb("ve", [P, CH])
        rstd = sb("rstd", [P, CH])
        xn = sb("xn", [P, CH, DM])
        xnt_h = sb("xnt_h", [P, KD, TOK], F32R)
        xnt_l = sb("xnt_l", [P, KD, TOK], F32R)
        sz = sb("sz", [P, 2, CH, DI])
        dt_raw = sb("dt_raw", [P, CH, H])
        raw = sb("raw", [P, 2, TAPS - 1 + TOK])
        halo = sb("halo", [P, NB, TAPS - 1])
        acc = sb("acc", [P, 2, TOK])
        xs = sb("xs", [P, 2, NB, TOK])
        c_h = sb("c_h", [P, 2, TOK], F32R)
        c_l = sb("c_l", [P, 2, TOK], F32R)
        v_dt = sb("v_dt", [P, CH, H])
        pos = sb("pos", [P, CH, H])
        nab = sb("nab", [P, CH, H])
        ex = sb("ex", [P, CH, H])
        den = sb("den", [P, CH, H])
        rcp = sb("rcp", [P, CH, H])
        ratio = sb("ratio", [P, CH, H])
        ratio2 = sb("ratio2", [P, CH, H])
        poly = sb("poly", [P, 2, CH, H])
        half_log = sb("half_log", [P, CH, H])
        dt = sb("dt", [P, CH, H])
        a_f = sb("a_f", [P, CH, H])
        a_h = sb("a_h", [P, CH, H], F32R)
        a_l = sb("a_l", [P, CH, H], F32R)
        ecs = sb("ecs", [P, 2, CH, H])
        v_h = sb("v_h", [P, 2, H, P], F32R)
        v_l = sb("v_l", [P, 2, H, P], F32R)
        decay = sb("decay", [P, CH, H, P])
        bt_h = sb("bt_h", [P, 2, NST], F32R)
        bt_l = sb("bt_l", [P, 2, NST], F32R)
        cbm = sb("cbm", [P, P])
        mix = sb("mix", [P, 2, H, P])
        xdt = sb("xdt", [P, 2, DI])
        xd = sb("xd", [P, 2, DI])
        xcd = sb("xcd", [P, DI])
        xcd_h = sb("xcd_h", [P, DI], F32R)
        xcd_l = sb("xcd_l", [P, DI], F32R)
        st = sb("st", [P, DI])
        st_h = sb("st_h", [P, DI], F32R)
        st_l = sb("st_l", [P, DI], F32R)
        y = sb("y", [P, 2, DI])
        squares = sb("squares", [P, DI])
        ssq = sb("ssq", [P, CH])
        mse = sb("mse", [P, CH])
        rms = sb("rms", [P, CH])
        yt_h = sb("yt_h", [P, 2, KI, P], F32R)
        yt_l = sb("yt_l", [P, 2, KI, P], F32R)
        u_res = sb("u_res", [P, 2, CH, DM])
        x1 = sb("x1", [P, 2, CH, DM])
        stage = decay[:, :, :, :].rearrange("p a b c -> p (a b c)")
        win_f = stage[:, 0:KD * WIN].rearrange("p (k n) -> p k n", k=KD)
        wo_f = stage[:, KD * WIN:KD * WIN + KI * DM].rearrange("p (k n) -> p k n", k=KI)

        bank = [ctx.enter_context(nc.psum_tensor(f"bank{i}", [P, 512], F32)) for i in range(8)]

        vec_in = sem("vec_in")
        win_in = sem("win_in")
        wo_in = sem("wo_in")
        const_step = sem("const_step")
        carrier = sem("carrier")
        consts = sem("consts")
        exp_a_ready = sem("exp_a_ready")
        wo_scaled = sem("wo_scaled")
        wh_ready = sem("wh_ready")
        wl_ready = sem("wl_ready")
        u_loaded = sem("u_loaded", 16)
        stats_ready = sem("stats_ready", CH)
        mv_ready = sem("mv_ready", CH)
        ve_ready = sem("ve_ready")
        rstd_ready = sem("rstd_ready")
        xn_ready = sem("xn_ready", CH)
        xnt_ps = sem("xnt_ps", KD)
        xnth_ready = sem("xnth_ready", KD)
        xntl_ready = sem("xntl_ready", KD)
        z_ps = sem("z_ps", 2 * CH)
        dt_copied = sem("dt_copied", CH)
        z_ready = sem("z_ready", 2 * CH)
        b_ps = sem("b_ps", NB)
        raw_ready = sem("raw_ready", NB)
        acc_ready = sem("acc_ready", NB)
        halo_in = sem("halo_in", NB)
        halo_out = sem("halo_out", NB, ahead=True)
        conv_step = sem("conv_step", 3 * NB, ahead=True)
        xs_ready = sem("xs_ready", NB)
        ch_ready = sem("ch_ready")
        cl_ready = sem("cl_ready")
        DT_NAB, DT_A, DT_ALL = 3, 17, 19
        dt_step = sem("dt_step", DT_ALL)
        ex_ready = sem("ex_ready")
        cs_ps = sem("cs_ps")
        ecs_ready = sem("ecs_ready")
        v_ready = sem("v_ready", 2 * CH)
        seg_ps = sem("seg_ps", 2 * CH)
        decay_ready = sem("decay_ready", 2 * CH)
        cb_ps = sem("cb_ps", CH)
        bth_ready = sem("bth_ready", CH)
        btl_ready = sem("btl_ready", CH)
        cbm_ready = sem("cbm_ready", CH, ahead=True)
        x_ps = sem("x_ps", CH)
        xdt_ready = sem("xdt_ready", CH)
        xd_ready = sem("xd_ready", CH, ahead=True)
        mix_ready = sem("mix_ready", CH)
        xcd_ready = sem("xcd_ready", CH)
        xcdh_ready = sem("xcdh_ready", CH)
        xcdl_ready = sem("xcdl_ready", CH)
        yo_ps = sem("yo_ps", CH)
        yd_ps = sem("yd_ps", CH)
        sp_ps = sem("sp_ps", CH, ahead=True)
        st_decayed = sem("st_decayed", CH)
        st_ready = sem("st_ready", CH, ahead=True)
        sth_ready = sem("sth_ready", CH, ahead=True)
        stl_ready = sem("stl_ready", CH, ahead=True)
        y_off = sem("y_off", CH, ahead=True)
        y_sum = sem("y_sum", CH, ahead=True)
        y_skip = sem("y_skip", CH)
        y_gated = sem("y_gated", CH)
        ssq_ready = sem("ssq_ready", CH)
        mse_ready = sem("mse_ready", CH)
        rms_ready = sem("rms_ready", CH)
        yt_ps = sem("yt_ps", CH)
        yth_ready = sem("yth_ready", CH)
        ytl_ready = sem("ytl_ready", CH)
        op_ps = sem("op_ps", CH)
        x1_ready = sem("x1_ready", CH, ahead=True)
        res_loaded = [sem("res_loaded0"), sem("res_loaded1")]
        x1_stored = [sem("x1_stored0"), sem("x1_stored1")]

        ORDER = ["A0", "Z0", "Z1", "Y0", "A1", "Z2", "T0", "Z3", "Y1", "A2", "O0", "B0", "T1",
                 "B1", "Y2", "A3", "O1", "B2", "T2", "B3", "Y3", "O2", "B4", "T3", "B5", "C0", "O3"]
        FRONT = [f"Z{c}" for c in range(CH)] + [f"B{b}" for b in range(NB)] + ["C0"]

        def step(piece, i, par, more):
            for name in ORDER:
                if more or name[0] in "AYTO":
                    piece(name[0], int(name[1]), i, par)

        def front_pieces(piece):
            for name in FRONT:
                piece(name[0], int(name[1]), -1, 1)

        block = ctx.enter_context(nc.Block())

        @block.sync
        def _(sp):
            def load_ln(n):
                need(sp, xn_ready, n - 1, CH)
                sp.dma_start(u_ln[:, :, :], u_v[n]).then_inc(u_loaded.handle, 16)

            def load_res(i, par):
                need(sp, x1_ready, 2 * i + par - 2, CH)
                sp.dma_start(u_res[:, par], u_v[2 * i + par]).then_inc(res_loaded[par].handle, 16)

            def store_x1(i, par):
                need(sp, x1_ready, 2 * i + par, CH)
                sp.dma_start(x1_d[2 * i + par], x1[:, par]).then_inc(x1_stored[par].handle, 16)

            load_ln(0)
            sp.dma_start(vecs[:, :], vec).then_inc(vec_in.handle, 16)
            for k in range(KD):
                sp.dma_start(win_f[:, k, :], win[:, k, :]).then_inc(win_in.handle, 16)
            sp.dma_start(wo_f, wo).then_inc(wo_in.handle, 16)
            load_res(0, 0)
            load_res(0, 1)
            load_ln(1)
            with sp.Fori(0, NS // 2 - 1) as i:
                for par in range(2):
                    load_ln(2 * i + par + 2)
                    store_x1(i, par)
                    load_res(i + 1, par)
            for par in range(2):
                store_x1(NS // 2 - 1, par)
            for par in range(2):
                sp.wait_ge(x1_stored[par].handle, 16 * (NS // 2 + 1))

        @block.tensor
        def _(pe):
            def transposes(n):
                for k in range(KD):
                    need(pe, xd_ready if k else cbm_ready, n - 2, CH)
                    for c in range(CH):
                        if k == 0:
                            need(pe, xn_ready, n, c + 1)
                        last = nc.tensor.transpose(bank[2 + k][:, c * P:(c + 1) * P],
                                                   xn[:, c, k * P:(k + 1) * P], ident[:, :])
                    sig(last, xnt_ps)

            def decays(s, more):
                if more:
                    transposes(s + 1)
                need(pe, y_off, s - 1, CH)
                need(pe, dt_step, s, DT_A)
                for k, mask in enumerate((ones, causal)):
                    last = nc.tensor.matmul(bank[4][:, k * CH * H:(k + 1) * CH * H], mask[:, :],
                                            flat(a_f[:, :, :]), start=True, stop=True)
                sig(last, cs_ps)
                for c in range(CH):
                    need(pe, v_ready, s, 2 * c + 2)
                    for g in range(2):
                        if c == 0:
                            need(pe, acc_ready, s, NB - 1 + g)
                        else:
                            need(pe, decay_ready, s, 2 * (c - 1) + g + 1)
                        hs = slice(g * H // 2, (g + 1) * H // 2)
                        nc.tensor.matmul(bank[g][:, :], after[:, :], flat(v_h[:, c % 2, hs]),
                                         start=True, stop=False)
                        sig(nc.tensor.matmul(bank[g][:, :], after[:, :], flat(v_l[:, c % 2, hs]),
                                             start=False, stop=True), seg_ps)

            def piece(kind, j, i, par):
                s = 2 * i + par
                n = s + 1
                tok = slice(j * P, (j + 1) * P)
                if kind == "Z":
                    if j == 0:
                        need(pe, xnth_ready, n, KD)
                        need(pe, xntl_ready, n, KD)
                    for g in range(2):
                        if j == 0:
                            need(pe, decay_ready, s, 2 * CH - 1 + g)
                        else:
                            need(pe, z_ready, n, 2 * (j - 1) + g + 1)
                        cols = slice(g * ZH, (g + 1) * ZH)
                        for k in range(KD):
                            last = product(nc, bank[g][:, 0:ZH], xnt_h[:, k, tok], xnt_l[:, k, tok],
                                           win_h[:, k, cols], win_l[:, k, cols], k == 0, k == KD - 1)
                        sig(last, z_ps)
                elif kind == "B":
                    g = j % 2
                    if j < 2:
                        need(pe, z_ready, n, 2 * (CH - 1) + g + 1)
                    else:
                        need(pe, acc_ready, n, j - 1)
                    cols = slice(ZD + j * P, ZD + (j + 1) * P)
                    for k in range(KD):
                        last = product(nc, bank[g][:, :], win_h[:, k, cols], win_l[:, k, cols],
                                       xnt_h[:, k, :], xnt_l[:, k, :], k == 0, k == KD - 1)
                    sig(last, b_ps)
                elif kind == "A":
                    if j == 0:
                        need(pe, xs_ready, s, NB)
                        if isinstance(s, int) and s == NS - 1:
                            need(pe, cbm_ready, s - 1, CH)
                            need(pe, xd_ready, s - 1, CH)
                        else:
                            need(pe, xntl_ready, n, KD)
                    else:
                        need(pe, cbm_ready, s, j)
                    nc.tensor.matmul(bank[2][:, 0:P], xs[:, par, IB, tok], xs[:, par, IC, tok],
                                     start=True, stop=True)
                    sig(nc.tensor.transpose(bank[2][:, P:2 * P], xs[:, par, IB, tok], ident[:, :]),
                        cb_ps)
                    if j:
                        need(pe, xd_ready, s, j)
                    for b in range(KI):
                        last = nc.tensor.transpose(bank[3][:, b * P:(b + 1) * P],
                                                   xs[:, par, b, tok], ident[:, :])
                    sig(last, x_ps)
                elif kind == "Y":
                    if j == 0:
                        need(pe, ch_ready, s, 1)
                        need(pe, cl_ready, s, 1)
                        need(pe, ecs_ready, s, 1)
                        need(pe, sth_ready, s - 1, CH)
                        need(pe, stl_ready, s - 1, CH)
                    else:
                        need(pe, y_off, s, j)
                        need(pe, sth_ready, s, j)
                        need(pe, stl_ready, s, j)
                    sig(product(nc, bank[4][:, :], c_h[:, par, tok], c_l[:, par, tok],
                                st_h[:, :], st_l[:, :], True, True), yo_ps)
                    need(pe, btl_ready, s, j + 1)
                    need(pe, xcdh_ready, s, j + 1)
                    need(pe, xcdl_ready, s, j + 1)
                    need(pe, st_ready, *((s, j) if j else (s - 1, CH)))
                    sig(product(nc, bank[6][:, :], bt_h[:, j % 2, :], bt_l[:, j % 2, :],
                                xcd_h[:, :], xcd_l[:, :], True, True), sp_ps)
                    need(pe, mix_ready, s, j + 1)
                    need(pe, xdt_ready, s, j + 1)
                    need(pe, y_sum, *((s, j) if j else (s - 1, CH)))
                    for h in range(H):
                        cols = slice(h * HD, min((h + 2) * HD, DI))
                        last = nc.tensor.matmul(bank[5][:, cols], mix[:, j % 2, h, :],
                                                xdt[:, j % 2, cols], start=True, stop=True)
                    sig(last, yd_ps)
                elif kind == "T":
                    need(pe, y_gated, s, j + 1)
                    need(pe, x1_ready, *((s, j) if j else (s - 1, CH)))
                    for b in range(KI):
                        last = nc.tensor.transpose(bank[7][:, b * P:(b + 1) * P],
                                                   y[:, j % 2, b * P:(b + 1) * P], ident[:, :])
                    sig(last, yt_ps)
                elif kind == "O":
                    need(pe, yth_ready, s, j + 1)
                    need(pe, ytl_ready, s, j + 1)
                    for b in range(KI):
                        last = product(nc, bank[7][:, 0:DM], yt_h[:, j % 2, b, :], yt_l[:, j % 2, b, :],
                                       wo_h[:, b, :], wo_l[:, b, :], b == 0, b == KI - 1)
                    sig(last, op_ps)

            credit(pe, sp_ps)
            pe.wait_ge(consts.handle, 3)
            transposes(0)
            pe.wait_ge(wh_ready.handle, 1)
            pe.wait_ge(wl_ready.handle, 1)
            front_pieces(piece)
            pe.wait_ge(wh_ready.handle, 2)
            pe.wait_ge(wl_ready.handle, 2)
            with pe.Fori(0, NS // 2 - 1) as i:
                for par in range(2):
                    decays(2 * i + par, True)
                    step(piece, i, par, True)
            decays(NS - 2, True)
            step(piece, NS // 2 - 1, 0, True)
            decays(NS - 1, False)
            step(piece, NS // 2 - 1, 1, False)

        @block.scalar
        def _(act):
            A = nc.scalar.activation

            def split_xnt(n):
                for k in range(KD):
                    need(act, xnt_ps, n, k + 1)
                    sig(A(xnt_h[:, k, :], bank[2 + k][:, :], ACT.Copy), xnth_ready)

            def decays(s, more):
                need(act, dt_step, s, DT_NAB)
                sig(A(ex[:, :, :], nab[:, :, :], ACT.Exp), ex_ready)
                if more:
                    split_xnt(s + 1)
                need(act, cs_ps, s, 1)
                sig(A(ecs[:, :, :, :].rearrange("p a c h -> p (a c h)"), bank[4][:, 0:2 * CH * H],
                      ACT.Exp), ecs_ready)
                for c in range(CH):
                    for g in range(2):
                        need(act, seg_ps, s, 2 * c + g + 1)
                        sig(A(flat(decay[:, c, g * H // 2:(g + 1) * H // 2]), bank[g][:, :], ACT.Exp),
                            decay_ready)

            def silu(n, npar, b):
                need(act, conv_step, n, 3 * (b + 1))
                sig(A(xs[:, npar, b, :], acc[:, b % 2, :], ACT.Silu), xs_ready)

            def piece(kind, j, i, par):
                s = 2 * i + par
                n, npar = s + 1, 1 - par
                if kind == "Z":
                    need(act, z_ps, n, 2 * j + 1)
                    sig(A(dt_raw[:, j, :], bank[0][:, 0:H], ACT.Copy), dt_copied)
                    sig(A(sz[:, npar, j, 0:ZH - H], bank[0][:, H:ZH], ACT.Silu), z_ready)
                    need(act, z_ps, n, 2 * j + 2)
                    sig(A(sz[:, npar, j, ZH - H:DI], bank[1][:, 0:ZH], ACT.Silu), z_ready)
                elif kind == "B":
                    g = j % 2
                    if j >= 2:
                        need(act, conv_step, n, 3 * (j - 1))
                        need(act, halo_out, n, j - 1)
                        need(act, xs_ready, n, j - 1)
                    else:
                        need(act, conv_step, n - 1, 3 * (NB - 1 + j))
                        need(act, halo_out, n - 1, NB - 1 + j)
                        need(act, xs_ready, n - 1, NB - 1 + j)
                    need(act, b_ps, n, j + 1)
                    sig(A(raw[:, g, TAPS - 1:], bank[g][:, :], ACT.Copy), raw_ready)
                    tap = V_TAP + j * TAPS + TAPS - 1
                    sig(A(acc[:, g, :], bank[g][:, :], ACT.Identity, bias=vecs[:, V_BIAS + j:V_BIAS + j + 1],
                          scale=vecs[:, tap:tap + 1]), acc_ready)
                    if j:
                        silu(n, npar, j - 1)
                elif kind == "C":
                    silu(n, npar, NB - 1)
                    need(act, xs_ready, n, NB)
                    sig(A(c_h[:, npar, :], xs[:, npar, IC, :], ACT.Copy), ch_ready)
                elif kind == "A":
                    need(act, cb_ps, s, j + 1)
                    sig(A(bt_h[:, j % 2, :], bank[2][:, P:2 * P], ACT.Copy), bth_ready)
                    need(act, xcd_ready, s, j + 1)
                    need(act, sp_ps, *((s, j) if j else (s - 1, CH)))
                    sig(A(xcd_h[:, :], xcd[:, :], ACT.Copy), xcdh_ready)
                elif kind == "Y":
                    need(act, st_ready, s, j + 1)
                    sig(A(st_h[:, :], st[:, :], ACT.Copy), sth_ready)
                elif kind == "T":
                    need(act, y_gated, s, j + 1)
                    sig(A(squares[:, :], y[:, j % 2, :], ACT.Square, accum_out=ssq[:, j:j + 1]),
                        ssq_ready)
                    need(act, yt_ps, s, j + 1)
                    sig(A(flat(yt_h[:, j % 2]), bank[7][:, :], ACT.Copy), yth_ready)

            credit(act, sth_ready)
            act.wait_ge(win_in.handle, 16 * KD)
            A(win_h[:, :, :], win_f, ACT.Copy).then_inc(wh_ready.handle, 1)
            split_xnt(0)
            act.wait_ge(vec_in.handle, 16)
            A(exp_a[:, :], vecs[:, V_A:V_A + H], ACT.Exp).then_inc(exp_a_ready.handle, 1)
            act.wait_ge(wo_scaled.handle, KI)
            A(wo_h[:, :, :], wo_f, ACT.Copy).then_inc(wh_ready.handle, 1)
            front_pieces(piece)
            with act.Fori(0, NS // 2 - 1) as i:
                for par in range(2):
                    decays(2 * i + par, True)
                    step(piece, i, par, True)
            decays(NS - 2, True)
            step(piece, NS // 2 - 1, 0, True)
            decays(NS - 1, False)
            step(piece, NS // 2 - 1, 1, False)

        @block.vector
        def _(dve):
            V = nc.vector

            def layer_norm(n):
                need(dve, u_loaded, n, 16)
                for c in range(CH):
                    sig(V.bn_stats(bst[:, c, :], u_ln[:, c, :]), stats_ready)
                for c in range(CH):
                    need_alone(dve, stats_ready, n, c + 1, carrier)
                    sig(V.bn_aggr(mv[:, c, :], bst[:, c, :]), mv_ready)
                need(dve, rstd_ready, n, 1)
                need(dve, xnt_ps, n - 1, KD)
                for c in range(CH):
                    sig(V.tensor_scalar(xn[:, c, :], u_ln[:, c, :], mv[:, c, 0:1], rstd[:, c:c + 1],
                                        ALU.subtract, ALU.mult), xn_ready)

            def split_xnt(n):
                for k in range(KD):
                    need(dve, xnth_ready, n, k + 1)
                    sig(V.tensor_tensor(xnt_l[:, k, :], bank[2 + k][:, :], xnt_h[:, k, :].bitcast(F32),
                                        ALU.subtract), xntl_ready)

            def decays(s, more):
                done = [0]

                def link(ins):
                    sig(ins, dt_step)
                    done[0] += 1
                    need(dve, dt_step, s, done[0])

                over_chunks = lambda ap: ap.unsqueeze(1).to_broadcast([P, CH, H])
                need(dve, dt_copied, s, CH)
                link(V.tensor_tensor(v_dt[:, :, :], dt_raw[:, :, :], over_chunks(vecs[:, V_DT:V_DT + H]),
                                     ALU.add))
                link(V.tensor_scalar(pos[:, :, :], v_dt[:, :, :], 0.0, None, ALU.max))
                link(V.scalar_tensor_tensor(nab[:, :, :], v_dt[:, :, :], -1.0, v_dt[:, :, :],
                                            ALU.mult, ALU.min))
                assert done[0] == DT_NAB
                need(dve, ex_ready, s, 1)
                link(V.tensor_scalar(den[:, :, :], ex[:, :, :], 2.0, None, ALU.add))
                link(V.reciprocal(rcp[:, :, :], den[:, :, :]))
                link(V.tensor_tensor(ratio[:, :, :], ex[:, :, :], rcp[:, :, :], ALU.mult))
                link(V.tensor_tensor(ratio2[:, :, :], ratio[:, :, :], ratio[:, :, :], ALU.mult))
                link(V.tensor_scalar(poly[:, 0], ratio2[:, :, :], 1.0 / 15, None, ALU.mult))
                for k, odd in enumerate((13, 11, 9, 7, 5, 3)):
                    link(V.scalar_tensor_tensor(poly[:, (k + 1) % 2], poly[:, k % 2], 1.0 / odd,
                                                ratio2[:, :, :], ALU.add, ALU.mult))
                link(V.scalar_tensor_tensor(half_log[:, :, :], poly[:, 0], 1.0, ratio[:, :, :],
                                            ALU.add, ALU.mult))
                link(V.scalar_tensor_tensor(dt[:, :, :], half_log[:, :, :], 2.0, pos[:, :, :],
                                            ALU.mult, ALU.add))
                link(V.scalar_tensor_tensor(a_f[:, :, :], dt[:, :, :], -1.0, over_chunks(exp_a[:, :]),
                                            ALU.mult, ALU.mult))
                assert done[0] == DT_A
                link(V.tensor_copy(a_h[:, :, :], a_f[:, :, :]))
                link(V.tensor_tensor(a_l[:, :, :], a_f[:, :, :], a_h[:, :, :].bitcast(F32), ALU.subtract))
                assert done[0] == DT_ALL
                if more:
                    split_xnt(s + 1)

            def heads(ap):
                return ap.rearrange("p (h d) -> p h d", h=H)

            def per_head(ap):
                return ap.unsqueeze(2).to_broadcast([P, H, HD])

            def piece(kind, j, i, par):
                s = 2 * i + par
                n = s + 1
                if kind == "B":
                    g = j % 2
                    need(dve, raw_ready, n, j + 1)
                    need(dve, halo_in, n, j + 1)
                    need(dve, acc_ready, n, j + 1)
                    for t in range(TAPS - 1):
                        if t:
                            need(dve, conv_step, n, 3 * j + t)
                        tap = V_TAP + j * TAPS + t
                        sig(V.scalar_tensor_tensor(acc[:, g, :], raw[:, g, t:t + TOK],
                                                   vecs[:, tap:tap + 1], acc[:, g, :],
                                                   ALU.mult, ALU.add), conv_step)
                elif kind == "A":
                    need(dve, bth_ready, s, j + 1)
                    sig(V.tensor_tensor(bt_l[:, j % 2, :], bank[2][:, P:2 * P],
                                        bt_h[:, j % 2, :].bitcast(F32), ALU.subtract), btl_ready)
                    sig(V.tensor_tensor(cbm[:, :], bank[2][:, 0:P], causal[:, :], ALU.mult), cbm_ready)
                    need(dve, x_ps, s, j + 1)
                    sig(V.tensor_tensor(heads(xdt[:, j % 2, :]), heads(bank[3][:, :]),
                                        per_head(dt[:, j, :]), ALU.mult), xdt_ready)
                    sig(V.tensor_tensor(heads(xd[:, j % 2, :]), heads(bank[3][:, :]),
                                        per_head(vecs[:, V_D:V_D + H]), ALU.mult), xd_ready)
                    need(dve, cbm_ready, s, j + 1)
                    need(dve, decay_ready, s, 2 * j + 2)
                    sig(V.tensor_tensor(mix[:, j % 2], decay[:, j],
                                        cbm[:, :].unsqueeze(1).to_broadcast([P, H, P]), ALU.mult),
                        mix_ready)
                elif kind == "Y":
                    need(dve, ecs_ready, s, 1)
                    need(dve, yo_ps, s, j + 1)
                    sig(V.tensor_tensor(heads(y[:, j % 2, :]), heads(bank[4][:, :]),
                                        per_head(ecs[:, 1, j, :]), ALU.mult), y_off)
                    need(dve, stl_ready, *((s, j) if j else (s - 1, CH)))
                    if par == SEQ - 1 and j == CH - 1:
                        sig(V.memset(st[:, :], 0.0), st_decayed)
                        need(dve, st_decayed, s, j + 1)
                        need(dve, sp_ps, s, j + 1)
                        sig(V.memset(st[:, 0:2], 0.0), st_ready)
                    else:
                        sig(V.tensor_tensor(heads(st[:, :]), heads(st[:, :]), per_head(ecs[:, 0, j, :]),
                                            ALU.mult), st_decayed)
                        need(dve, st_decayed, s, j + 1)
                        need(dve, sp_ps, s, j + 1)
                        sig(V.tensor_tensor(st[:, :], st[:, :], bank[6][:, :], ALU.add), st_ready)
                    need(dve, y_off, s, j + 1)
                    need(dve, yd_ps, s, j + 1)
                    sig(V.tensor_tensor(y[:, j % 2, :], y[:, j % 2, :], bank[5][:, :], ALU.add), y_sum)
                elif kind == "T":
                    need(dve, y_skip, s, j + 1)
                    sig(V.tensor_tensor(y[:, j % 2, :], y[:, j % 2, :], sz[:, par, j, :], ALU.mult),
                        y_gated)
                    need(dve, yth_ready, s, j + 1)
                    sig(V.tensor_tensor(flat(yt_l[:, j % 2]), bank[7][:, :],
                                        flat(yt_h[:, j % 2]).bitcast(F32), ALU.subtract), ytl_ready)
                elif kind == "O":
                    if j == 0:
                        dve.wait_ge(res_loaded[par].handle, 16 * (i + 1))
                        dve.wait_ge(x1_stored[par].handle, 16 * (i + 1))
                    need(dve, rms_ready, s, j + 1)
                    need(dve, op_ps, s, j + 1)
                    sig(V.scalar_tensor_tensor(x1[:, par, j, :], bank[7][:, 0:DM], rms[:, j:j + 1],
                                               u_res[:, par, j, :], ALU.mult, ALU.add), x1_ready)

            credit(dve, conv_step, cbm_ready, xd_ready, st_ready, y_off, y_sum, x1_ready)
            for par in range(2):
                dve.sem_inc(x1_stored[par].handle, 16)
            V.memset(st[:, :], 0.0).then_inc(consts.handle, 1)
            layer_norm(0)
            dve.wait_ge(wh_ready.handle, 1)
            V.tensor_tensor(win_l[:, :, :], win_f, win_h[:, :, :].bitcast(F32), ALU.subtract)\
                .then_inc(wl_ready.handle, 1)
            split_xnt(0)
            dve.wait_ge(vec_in.handle, 16)
            dve.wait_ge(wo_in.handle, 16)
            for b in range(KI):
                V.tensor_scalar(wo_f[:, b, :], wo_f[:, b, :], vecs[:, V_NORM + b:V_NORM + b + 1], None,
                                ALU.mult).then_inc(wo_scaled.handle, 1)
            dve.wait_ge(wh_ready.handle, 2)
            V.tensor_tensor(wo_l[:, :, :], wo_f, wo_h[:, :, :].bitcast(F32), ALU.subtract)\
                .then_inc(wl_ready.handle, 1)
            dve.wait_ge(exp_a_ready.handle, 1)
            dve.wait_ge(consts.handle, 3)
            front_pieces(piece)
            layer_norm(1)
            with dve.Fori(0, NS // 2 - 1) as i:
                for par in range(2):
                    decays(2 * i + par, True)
                    step(piece, i, par, True)
                    layer_norm(2 * i + par + 2)
            decays(NS - 2, True)
            step(piece, NS // 2 - 1, 0, True)
            decays(NS - 1, False)
            step(piece, NS // 2 - 1, 1, False)

        @block.gpsimd
        def _(pool):
            G = nc.gpsimd

            def rstd_of(n):
                need_alone(pool, mv_ready, n, CH, carrier)
                sig(G.tensor_scalar(ve[:, :], mv[:, :, 1], EPS, None, ALU.add), ve_ready)
                need(pool, ve_ready, n, 1)
                sig(G.tensor_tensor(rstd[:, :], ve[:, :], neg_half[:, :], ALU.pow), rstd_ready)

            def decays(s):
                need(pool, dt_step, s, DT_ALL)
                for c in range(CH):
                    if c >= 2:
                        need(pool, seg_ps, s, 2 * (c - 1))
                    for dst, src in ((v_h, a_h), (v_l, a_l)):
                        sig(G.tensor_tensor(
                            dst[:, c % 2], causal[:, :].unsqueeze(1).to_broadcast([P, H, P]),
                            src[:, c, :].bitcast(F32).unsqueeze(2).to_broadcast([P, H, P]),
                            ALU.mult), v_ready)

            def piece(kind, j, i, par):
                s = 2 * i + par
                n, npar = s + 1, 1 - par
                if kind == "B":
                    g = j % 2
                    need_alone(pool, conv_step,
                               *((n, 3 * (j - 1)) if j >= 2 else (n - 1, 3 * (NB - 1 + j))), carrier)
                    if npar == 0:
                        sig(G.memset(raw[:, g, 0:TAPS - 1], 0.0), halo_in)
                    else:
                        need_alone(pool, halo_out, n - 1, j + 1, carrier)
                        sig(G.tensor_copy(raw[:, g, 0:TAPS - 1], halo[:, j, :]), halo_in)
                    need(pool, halo_in, n, j + 1)
                    need_alone(pool, raw_ready, n, j + 1, carrier)
                    sig(G.tensor_copy(halo[:, j, :], raw[:, g, TOK:TOK + TAPS - 1]), halo_out)
                elif kind == "C":
                    need(pool, ch_ready, n, 1)
                    sig(G.tensor_tensor(c_l[:, npar, :], xs[:, npar, IC, :],
                                        c_h[:, npar, :].bitcast(F32), ALU.subtract), cl_ready)
                elif kind == "A":
                    need(pool, xdt_ready, s, j + 1)
                    need(pool, decay_ready, s, 2 * j + 2)
                    sig(G.tensor_tensor(xcd[:, :].rearrange("p (h d) -> p h d", h=H),
                                        xdt[:, j % 2, :].rearrange("p (h d) -> p h d", h=H),
                                        decay[:, j, :, P - 1:P].to_broadcast([P, H, HD]), ALU.mult),
                        xcd_ready)
                    need(pool, xcdh_ready, s, j + 1)
                    sig(G.tensor_tensor(xcd_l[:, :], xcd[:, :], xcd_h[:, :].bitcast(F32),
                                        ALU.subtract), xcdl_ready)
                elif kind == "Y":
                    need(pool, sth_ready, s, j + 1)
                    sig(G.tensor_tensor(st_l[:, :], st[:, :], st_h[:, :].bitcast(F32), ALU.subtract),
                        stl_ready)
                    need(pool, y_sum, s, j + 1)
                    sig(G.tensor_tensor(y[:, j % 2, :], y[:, j % 2, :], xd[:, j % 2, :], ALU.add), y_skip)
                elif kind == "T":
                    need_alone(pool, ssq_ready, s, j + 1, carrier)
                    sig(G.tensor_scalar(mse[:, j:j + 1], ssq[:, j:j + 1], 1.0 / DI, EPS,
                                        ALU.mult, ALU.add), mse_ready)
                    need(pool, mse_ready, s, j + 1)
                    sig(G.tensor_tensor(rms[:, j:j + 1], mse[:, j:j + 1], neg_half[:, 0:1], ALU.pow),
                        rms_ready)

            credit(pool, halo_out, stl_ready)
            for m, value in ((ident, 0.0), (causal, 1.0), (after_f, 1.0), (ones, 1.0), (neg_half, -0.5)):
                G.memset(m[:, :], value).then_inc(const_step.handle, 1)
            for m in (st_h, st_l):
                G.memset(m[:, :].bitcast(F32), 0.0).then_inc(const_step.handle, 1)
            pool.wait_ge(const_step.handle, 7)
            for m, op, fill, a, b in ((ident, ALU.not_equal, 1.0, -1, 1), (causal, ALU.is_ge, 0.0, 1, -1),
                                      (after_f, ALU.is_gt, 0.0, -1, 1)):
                G.affine_select(out=m[:, :], in_=m[:, :], compare_op=op, fill=fill, base=0,
                                pattern=[[a, P]], channel_multiplier=b).then_inc(const_step.handle, 1)
            pool.wait_ge(const_step.handle, 10)
            G.tensor_copy(after[:, :], after_f[:, :]).then_inc(const_step.handle, 1)
            pool.wait_ge(const_step.handle, 11)
            G.memset(halo[:, :, :], 0.0).then_inc(consts.handle, 2)
            rstd_of(0)
            front_pieces(piece)
            rstd_of(1)
            with pool.Fori(0, NS // 2 - 1) as i:
                for par in range(2):
                    decays(2 * i + par)
                    step(piece, i, par, True)
                    rstd_of(2 * i + par + 2)
            decays(NS - 2)
            step(piece, NS // 2 - 1, 0, True)
            decays(NS - 1)
            step(piece, NS // 2 - 1, 1, False)


def experts(nc, NS, x1_d, w1, w3, w2, out_v):
    ctx = ExitStack()
    with ctx:
        def sb(name, shape, dt=F32):
            return ctx.enter_context(nc.sbuf_tensor(name, shape, dt))

        def sem(name, per=1, ahead=False):
            return Count(ctx.enter_context(nc.semaphore(name)), per, ahead)

        w1_f = sb("w1_f", [P, FB, KD * P])
        w3_f = sb("w3_f", [P, FB, KD * P])
        w2_f = sb("w2_f", [P, FB, DM])
        w1_h = sb("w1_h", [P, FB, KD * P], F32R)
        w1_l = sb("w1_l", [P, FB, KD * P], F32R)
        w3_h = sb("w3_h", [P, FB, KD * P], F32R)
        w3_l = sb("w3_l", [P, FB, KD * P], F32R)
        w2_h = sb("w2_h", [P, FB, DM], F32R)
        w2_l = sb("w2_l", [P, FB, DM], F32R)
        ident = sb("ident2", [P, P])
        sel_f = sb("sel_f", [2 * E, 2, P])
        sel = sb("sel", [2 * E, P], F32R)
        neg_half = sb("neg_half2", [P, CH])
        rank = sb("rank", [P, E])
        x1 = sb("x1_in", [P, 2, CH, DM])
        bst = sb("bst2", [P, CH, 6])
        mv = sb("mv2", [P, CH, 2])
        ve = sb("ve2", [P, CH])
        rstd = sb("rstd2", [P, CH])
        xn = sb("xn2", [P, CH, DM])
        xt_h = sb("xt_h", [P, 2, KD, TOK], F32R)
        xt_l = sb("xt_l", [P, 2, KD, TOK], F32R)
        lg = sb("lg", [P, TOK])
        lgt = sb("lgt", [P, CH, E])
        shifted = sb("shifted", [P, CH, E])
        ep = sb("ep", [P, CH, E])
        score = sb("score", [P, CH, E])
        top = sb("top", [P, CH])
        total = sb("total", [P, CH])
        inv = sb("inv", [P, CH])
        tied = sb("tied", [P, CH, E])
        tied_rank = sb("tied_rank", [P, CH, E])
        best_rank = sb("best_rank", [P, CH])
        pick1 = sb("pick1", [P, CH, E])
        pick2 = sb("pick2", [P, CH, E])
        rest = sb("rest", [P, CH, E])
        cw = sb("cw", [P, CH, E])
        cw_r = sb("cw_r", [P, CH, E], F32R)
        cw_parts = sb("cw_parts", [P, CH, 2 * E])
        cwt = sb("cwt", [2 * E, TOK], F32R)
        cwb = sb("cwb", [P, TOK])
        act1 = sb("act1", [P, 2, TOK])
        g = sb("g", [P, 2, TOK])
        g_h = sb("g_h", [P, 2, TOK], F32R)
        g_l = sb("g_l", [P, 2, TOK], F32R)
        y2t = sb("y2t", [P, KD, TOK])
        ob = sb("ob", [P, CH, DM])
        bank = [ctx.enter_context(nc.psum_tensor(f"ebank{k}", [P, 512], F32)) for k in range(8)]

        w_in = [sem(f"w_in{k}") for k in range(len(GROUPS))]
        wh_ready = sem("e_wh_ready")
        wl_ready = sem("e_wl_ready")
        const_step = sem("e_const_step")
        carrier = sem("e_carrier")
        consts = sem("e_consts")
        x1_loaded = [sem("x1_loaded0"), sem("x1_loaded1")]
        stats_ready = sem("e_stats_ready", CH)
        mv_ready = sem("e_mv_ready", CH)
        ve_ready = sem("e_ve_ready")
        rstd_ready = sem("e_rstd_ready")
        xn_ready = sem("e_xn_ready", CH)
        xt_ps = sem("xt_ps", KD)
        xth_ready = sem("xth_ready", KD)
        xtl_ready = sem("xtl_ready", KD)
        h1_ps = sem("h1_ps", FB)
        h3_ps = sem("h3_ps", FB)
        act_ready = sem("act_ready", FB)
        lg_ready = sem("lg_ready")
        lg_ps = sem("lg_ps")
        lgt_ready = sem("lgt_ready")
        R_SHIFT, R_ALL = 2, 21
        route = sem("route", R_ALL)
        ep_ready = sem("ep_ready")
        cwt_ps = sem("cwt_ps")
        cwt_ready = sem("cwt_ready")
        cwb_ps = sem("cwb_ps")
        cwb_ready = sem("cwb_ready")
        prod_ready = sem("prod_ready", FB)
        g_ready = sem("g_ready", RB)
        gh_ready = sem("gh_ready", FB)
        gl_ready = sem("gl_ready", FB)
        down_ps = sem("down_ps", FB)
        y2_ready = sem("y2_ready", KD)
        ot_ps = sem("ot_ps", 2)
        ob_ready = sem("ob_ready", 2)
        stored = sem("stored", 16, ahead=True)

        ORDER = ["F0", "H0", f"D{FB - 1}", "K0", "G0", "F1", "H1", "D0", "Q0", "F2", "H2", "D1",
                 "C0", "F3", "S0", "H3", "D2"]
        for j in range(4, FB):
            ORDER += [f"F{j}", f"H{j}"] + (["L0"] if j == 5 else []) + (["X0"] if j == 9 else [])
            ORDER += [f"D{j - 1}"]

        def step(piece, n, par, loads, first, last):
            for name in ORDER:
                kind, j = name[0], int(name[1:])
                before = kind in "KQ" or name == f"D{FB - 1}"
                if (before and first) or (kind in "LX" and last):
                    continue
                piece(kind, j, n - 1 if before else n, 1 - par if before else par,
                      loads if kind == "L" else None, first)

        def run(eng, piece):
            step(piece, 0, 0, 1, True, False)
            with eng.Fori(0, NS // 2 - 1) as i:
                step(piece, 2 * i + 1, 1, i + 2, False, False)
                step(piece, 2 * i + 2, 0, i + 2, False, False)
            step(piece, NS - 1, 1, None, False, True)
            for kind, j in (("D", FB - 1), ("K", 0), ("Q", 0)):
                piece(kind, j, NS - 1, 1, None, False)

        block = ctx.enter_context(nc.Block())

        @block.sync
        def _(sp):
            def load(n, par):
                need(sp, ob_ready, n - 2, 2)
                sp.dma_start(x1[:, par], x1_d[n]).then_inc(x1_loaded[par].handle, 16)

            def store(n):
                need(sp, ob_ready, n, 2)
                sp.dma_start(out_v[n], ob[:, :, :]).then_inc(stored.handle, 16)

            credit(sp, stored)
            load(0, 0)
            for k, (a, b) in enumerate(GROUPS):
                for dst, src in ((w1_f, w1), (w3_f, w3), (w2_f, w2)):
                    sp.dma_start(dst[:, a:b, :], src[:, a:b, :]).then_inc(w_in[k].handle, 16)
            load(1, 1)
            with sp.Fori(0, NS // 2 - 1) as i:
                for par in range(2):
                    store(2 * i + par)
                    load(2 * i + par + 2, par)
            store(NS - 2)
            store(NS - 1)
            need(sp, stored, NS - 1, 16)

        @block.tensor
        def _(pe):
            def transposes(n, par):
                for k in range(KD):
                    for c in range(CH):
                        if k == 0:
                            need(pe, xn_ready, n, c + 1)
                        last = nc.tensor.transpose(bank[6 + k][:, c * P:(c + 1) * P],
                                                   xn[:, c, k * P:(k + 1) * P], ident[:, :])
                    sig(last, xt_ps)

            def piece(kind, j, n, par, loads, first):
                if kind == "F":
                    b = j % 2
                    if j == 0:
                        need(pe, xth_ready, n, KD)
                        need(pe, xtl_ready, n, KD)
                    if first:
                        for k, (a, _) in enumerate(GROUPS):
                            if a == j:
                                pe.wait_ge(wh_ready.handle, 3 * (k + 1))
                                pe.wait_ge(wl_ready.handle, 3 * (k + 1))
                    need(pe, act_ready, *((n, j - 1) if j >= 2 else (n - 1, FB - 1 + j)))
                    if j == 2:
                        need(pe, lg_ready, n, 1)
                    for k in range(KD):
                        cols = slice(k * P, (k + 1) * P)
                        last = product(nc, bank[2 + b][:, :], w1_h[:, j, cols], w1_l[:, j, cols],
                                       xt_h[:, par, k, :], xt_l[:, par, k, :], k == 0, k == KD - 1)
                    sig(last, h1_ps)
                    need(pe, prod_ready, *((n, j - 1) if j >= 2 else (n - 1, FB - 1 + j)))
                    for k in range(KD):
                        cols = slice(k * P, (k + 1) * P)
                        last = product(nc, bank[4 + b][:, :], w3_h[:, j, cols], w3_l[:, j, cols],
                                       xt_h[:, par, k, :], xt_l[:, par, k, :], k == 0, k == KD - 1)
                    sig(last, h3_ps)
                elif kind == "D":
                    need(pe, gh_ready, n, j + 1)
                    need(pe, gl_ready, n, j + 1)
                    if j == 0:
                        need(pe, y2_ready, n - 1, KD)
                    for k in range(KD):
                        cols = slice(k * P, (k + 1) * P)
                        last = product(nc, bank[k][:, :], w2_h[:, j, cols], w2_l[:, j, cols],
                                       g_h[:, j % 2, :], g_l[:, j % 2, :], j == 0, j == FB - 1)
                    sig(last, down_ps)
                elif kind == "G":
                    need(pe, lg_ready, n, 1)
                    need_alone(pe, xtl_ready, n, KD, carrier)
                    for c in range(CH):
                        last = nc.tensor.transpose(bank[6][:, c * 32:(c + 1) * 32],
                                                   lg[GROW:P, c * P:(c + 1) * P], ident[GROW:P, GROW:P])
                    sig(last, lg_ps)
                elif kind == "C":
                    need(pe, route, n, R_ALL)
                    if not first:
                        need(pe, ob_ready, n - 1, 2)
                    for c in range(CH):
                        last = nc.tensor.transpose(bank[7][0:2 * E, c * P:(c + 1) * P],
                                                   cw_parts[:, c, :], ident[:, :])
                    sig(last, cwt_ps)
                elif kind == "S":
                    need(pe, cwt_ready, n, 1)
                    if not first:
                        need(pe, ob_ready, n - 1, 1)
                    need(pe, lgt_ready, n, 1)
                    sig(nc.tensor.matmul(bank[6][:, :], sel[:, :], cwt[:, :], start=True, stop=True), cwb_ps)
                elif kind == "Q":
                    need(pe, y2_ready, n, KD)
                    if isinstance(n, int) and n == NS - 1:
                        need(pe, cwb_ready, n, 1)
                    else:
                        need(pe, lgt_ready, n + 1, 1)
                    for t in range(2):
                        for c in range(2):
                            tok = slice((2 * t + c) * P, (2 * t + c + 1) * P)
                            for k in range(KD):
                                at = c * DM + k * P
                                last = nc.tensor.transpose(bank[6 + t][:, at:at + P], y2t[:, k, tok],
                                                           ident[:, :])
                        sig(last, ot_ps)
                elif kind == "X":
                    need(pe, cwb_ready, n, 1)
                    transposes(n + 1, 1 - par)

            pe.wait_ge(consts.handle, 1)
            transposes(0, 0)
            run(pe, piece)

        @block.scalar
        def _(act):
            A = nc.scalar.activation

            def split_xt(n, par):
                for k in range(KD):
                    need(act, xt_ps, n, k + 1)
                    sig(A(xt_h[:, par, k, :], bank[6 + k][:, :], ACT.Copy), xth_ready)

            def split_weights(k):
                a, b = GROUPS[k]
                act.wait_ge(w_in[k].handle, 48)
                for dst, src in ((w1_h, w1_f), (w3_h, w3_f), (w2_h, w2_f)):
                    sig(A(dst[:, a:b, :], src[:, a:b, :], ACT.Copy), wh_ready)

            def piece(kind, j, n, par, loads, first):
                if kind == "F":
                    need(act, h1_ps, n, j + 1)
                    need(act, prod_ready, *((n, j - 1) if j >= 2 else (n - 1, FB - 1 + j)))
                    sig(A(act1[:, j % 2, :], bank[2 + j % 2][:, :], ACT.Silu), act_ready)
                    if j == 0:
                        sig(A(lg[GROW:P, :], bank[2][GROW:P, :], ACT.Copy), lg_ready)
                    if first:
                        for k, (a, _) in enumerate(GROUPS):
                            if a == j + 2 and k:
                                split_weights(k)
                elif kind == "H":
                    if j < SB:
                        need(act, prod_ready, n, j + 1)
                    else:
                        need(act, g_ready, n, j - SB + 1)
                    need(act, down_ps, *((n, j - 1) if j >= 2 else (n - 1, FB - 1 + j)))
                    sig(A(g_h[:, j % 2, :], g[:, j % 2, :], ACT.Copy), gh_ready)
                elif kind == "G":
                    need(act, lg_ps, n, 1)
                    sig(A(lgt[:, :, :], bank[6][:, 0:CH * 32].rearrange("p (c e) -> p c e", c=CH)[:, :, 0:E],
                          ACT.Copy), lgt_ready)
                    need(act, route, n, R_SHIFT)
                    sig(A(ep[:, :, :], shifted[:, :, :], ACT.Exp), ep_ready)
                elif kind == "C":
                    need(act, cwt_ps, n, 1)
                    sig(A(cwt[:, :], bank[7][0:2 * E, :], ACT.Copy), cwt_ready)
                elif kind == "S":
                    need(act, cwb_ps, n, 1)
                    sig(A(cwb[:, :], bank[6][:, :], ACT.Copy), cwb_ready)
                elif kind == "K":
                    need(act, down_ps, n, FB)
                    for k in range(KD):
                        sig(A(y2t[:, k, :], bank[k][:, :], ACT.Copy), y2_ready)
                elif kind == "X":
                    split_xt(n + 1, 1 - par)

            split_weights(0)
            split_xt(0, 0)
            run(act, piece)

        @block.vector
        def _(dve):
            V = nc.vector

            def layer_norm(n, par, loads):
                dve.wait_ge(x1_loaded[par].handle, 16 * loads)
                for c in range(CH):
                    sig(V.bn_stats(bst[:, c, :], x1[:, par, c, :]), stats_ready)
                for c in range(CH):
                    need_alone(dve, stats_ready, n, c + 1, carrier)
                    sig(V.bn_aggr(mv[:, c, :], bst[:, c, :]), mv_ready)
                need(dve, rstd_ready, n, 1)
                need(dve, xt_ps, n - 1, KD)
                for c in range(CH):
                    sig(V.tensor_scalar(xn[:, c, :], x1[:, par, c, :], mv[:, c, 0:1], rstd[:, c:c + 1],
                                        ALU.subtract, ALU.mult), xn_ready)

            def split_xt(n, par):
                for k in range(KD):
                    need(dve, xth_ready, n, k + 1)
                    sig(V.tensor_tensor(xt_l[:, par, k, :], bank[6 + k][:, :],
                                        xt_h[:, par, k, :].bitcast(F32), ALU.subtract), xtl_ready)

            def split_weights(k):
                a, b = GROUPS[k]
                for m, (dst, src, hi) in enumerate(((w1_l, w1_f, w1_h), (w3_l, w3_f, w3_h),
                                                    (w2_l, w2_f, w2_h))):
                    dve.wait_ge(wh_ready.handle, 3 * k + m + 1)
                    sig(V.tensor_tensor(dst[:, a:b, :], src[:, a:b, :], hi[:, a:b, :].bitcast(F32),
                                        ALU.subtract), wl_ready)

            def routing(n):
                done = [0]

                def link(ins):
                    sig(ins, route)
                    done[0] += 1
                    need(dve, route, n, done[0])

                per_tok = lambda ap: ap.unsqueeze(2).to_broadcast([P, CH, E])
                ranks = rank[:, :].unsqueeze(1).to_broadcast([P, CH, E])
                need(dve, lgt_ready, n, 1)
                link(V.tensor_reduce(top[:, :], lgt[:, :, :], AX.X, ALU.max))
                link(V.tensor_tensor(shifted[:, :, :], lgt[:, :, :], per_tok(top[:, :]), ALU.subtract))
                assert done[0] == R_SHIFT
                need(dve, ep_ready, n, 1)
                link(V.tensor_reduce(total[:, :], ep[:, :, :], AX.X, ALU.add))
                link(V.reciprocal(inv[:, :], total[:, :]))
                link(V.tensor_tensor(score[:, :, :], ep[:, :, :], per_tok(inv[:, :]), ALU.mult))
                for left, pick in ((score, pick1), (rest, pick2)):
                    link(V.tensor_reduce(top[:, :], left[:, :, :], AX.X, ALU.max))
                    link(V.tensor_tensor(tied[:, :, :], left[:, :, :], per_tok(top[:, :]), ALU.is_equal))
                    link(V.tensor_tensor(tied_rank[:, :, :], tied[:, :, :], ranks, ALU.mult))
                    link(V.tensor_reduce(best_rank[:, :], tied_rank[:, :, :], AX.X, ALU.max))
                    link(V.tensor_tensor(pick[:, :, :], tied_rank[:, :, :], per_tok(best_rank[:, :]),
                                         ALU.is_equal))
                    if pick is pick1:
                        link(V.scalar_tensor_tensor(rest[:, :, :], pick1[:, :, :], -2.0, score[:, :, :],
                                                    ALU.mult, ALU.add))
                link(V.tensor_tensor(tied[:, :, :], pick1[:, :, :], pick2[:, :, :], ALU.add))
                link(V.tensor_tensor(cw[:, :, :], score[:, :, :], tied[:, :, :], ALU.mult))
                link(V.tensor_copy(cw_r[:, :, :], cw[:, :, :]))
                link(V.tensor_copy(cw_parts[:, :, 0:E], cw_r[:, :, :].bitcast(F32)))
                link(V.tensor_tensor(cw_parts[:, :, E:2 * E], cw[:, :, :], cw_r[:, :, :].bitcast(F32),
                                     ALU.subtract))
                assert done[0] == R_ALL

            def piece(kind, j, n, par, loads, first):
                if kind == "F":
                    need(dve, act_ready, n, j + 1)
                    need(dve, h3_ps, n, j + 1)
                    need(dve, gl_ready, *((n, j - 1) if j >= 2 else (n - 1, FB - 1 + j)))
                    sig(V.tensor_tensor(g[:, j % 2, :], bank[4 + j % 2][:, :], act1[:, j % 2, :], ALU.mult),
                        prod_ready)
                    if first:
                        for k, (a, _) in enumerate(GROUPS):
                            if a == j + 2 and k:
                                split_weights(k)
                elif kind == "G":
                    routing(n)
                elif kind == "H" and j >= SB:
                    if j == SB:
                        need(dve, cwb_ready, n, 1)
                    need(dve, prod_ready, n, j + 1)
                    sig(V.tensor_tensor(g[:, j % 2, :], g[:, j % 2, :], cwb[:, :], ALU.mult), g_ready)
                elif kind == "Q":
                    need(dve, stored, n - 1, 16)
                    for t in range(2):
                        need(dve, ot_ps, n, t + 1)
                        sig(V.tensor_tensor(flat(ob[:, 2 * t:2 * t + 2, :]), bank[6 + t][:, :],
                                            flat(x1[:, par, 2 * t:2 * t + 2, :]), ALU.add), ob_ready)
                elif kind == "L":
                    layer_norm(n + 1, 1 - par, loads)
                elif kind == "X":
                    split_xt(n + 1, 1 - par)

            layer_norm(0, 0, 1)
            split_weights(0)
            split_xt(0, 0)
            run(dve, piece)

        @block.gpsimd
        def _(pool):
            G = nc.gpsimd

            def rstd_of(n):
                need_alone(pool, mv_ready, n, CH, carrier)
                sig(G.tensor_scalar(ve[:, :], mv[:, :, 1], EPS, None, ALU.add), ve_ready)
                need(pool, ve_ready, n, 1)
                sig(G.tensor_tensor(rstd[:, :], ve[:, :], neg_half[:, :], ALU.pow), rstd_ready)

            def piece(kind, j, n, par, loads, first):
                if kind == "H":
                    need(pool, gh_ready, n, j + 1)
                    sig(G.tensor_tensor(g_l[:, j % 2, :], g[:, j % 2, :], g_h[:, j % 2, :].bitcast(F32),
                                        ALU.subtract), gl_ready)
                elif kind == "L":
                    rstd_of(n + 1)

            const = [0]

            def made(ins):
                ins.then_inc(const_step.handle, 1)
                const[0] += 1

            made(G.memset(ident[:, :], 0.0))
            made(G.memset(neg_half[:, :], -0.5))
            made(G.memset(sel_f[:, :, :], 1.0))
            for e in range(E):
                made(G.memset(rank[:, e:e + 1], float(E - e)))
            pool.wait_ge(const_step.handle, const[0])
            made(G.affine_select(out=ident[:, :], in_=ident[:, :], compare_op=ALU.not_equal, fill=1.0,
                                 base=0, pattern=[[-1, P]], channel_multiplier=1))
            wide = P // E
            for k in range(2):
                made(G.affine_select(out=sel_f[:, k, :], in_=sel_f[:, k, :], compare_op=ALU.is_ge, fill=0.0,
                                     base=k * P, pattern=[[1, P]], channel_multiplier=-wide))
            pool.wait_ge(const_step.handle, const[0])
            for k in range(2):
                made(G.affine_select(out=sel_f[:, k, :], in_=sel_f[:, k, :], compare_op=ALU.is_ge, fill=0.0,
                                     base=wide - 1 - k * P, pattern=[[-1, P]], channel_multiplier=wide))
            pool.wait_ge(const_step.handle, const[0])
            G.tensor_tensor(sel[:, :], sel_f[:, 0, :], sel_f[:, 1, :], ALU.add).then_inc(consts.handle, 1)
            rstd_of(0)
            run(pool, piece)


def build(nc, u, win, wo, vec, w1, w3, w2, out):
    NS = u.shape[0] * u.shape[1] // TOK
    u_v = u.rearrange("b (n c p) d -> (b n) p c d", c=CH, p=P)
    out_v = out.rearrange("b (n c p) d -> (b n) p c d", c=CH, p=P)
    x1_d = nc.dram_tensor("x1_between_phases", (NS, P, CH, DM), F32).ap()
    mixer(nc, NS, u_v, win, wo, vec, x1_d)
    experts(nc, NS, x1_d, w1, w3, w2, out_v)


def kernel(**inputs):
    import numpy as np
    import concourse.bacc as bacc
    from concourse.bass_utils import run_bass_kernel_spmd

    x = {k: np.asarray(v) for k, v in inputs.items()}
    f32 = np.float32
    u = np.ascontiguousarray(x["L0_attn_u"])

    w = x["L0_attn_in_proj_w"].T
    w = np.concatenate([w[:, DI + XBC:], w[:, :DI], w[:, DI:DI + XBC]], axis=1)
    win = np.ascontiguousarray(w.reshape(KD, P, WIN).transpose(1, 0, 2))
    wo = np.ascontiguousarray(x["L0_attn_out_proj_w"].T.reshape(KI, P, DM).transpose(1, 0, 2))

    vec = np.zeros((P, V_ALL), f32)
    vec[:, V_TAP:V_BIAS] = x["L0_attn_conv_w"].reshape(NB, P, TAPS).transpose(1, 0, 2).reshape(P, -1)
    vec[:, V_BIAS:V_NORM] = x["L0_attn_conv_b"].reshape(NB, P).T
    vec[:, V_NORM:V_DT] = x["L0_attn_norm_w"].reshape(KI, P).T
    vec[:, V_DT:V_A] = x["L0_attn_dt_bias"]
    vec[:, V_A:V_D] = x["L0_attn_A_log"]
    vec[:, V_D:] = x["L0_attn_D"]

    def up(shared, routed, gate=None):
        cols = np.zeros((DM, FB, P), f32)
        cols[:, 0, :GROW] = shared[:, (SB - 1) * P:]
        cols[:, 1:SB] = shared[:, :(SB - 1) * P].reshape(DM, SB - 1, P)
        if gate is not None:
            cols[:, 0, GROW:GROW + E] = gate
        cols[:, SB:] = routed.transpose(1, 0, 2).reshape(DM, E, RB, FE // RB).transpose(0, 2, 1, 3)\
            .reshape(DM, RB, P)
        return np.ascontiguousarray(cols.reshape(KD, P, FB, P).transpose(1, 2, 0, 3).reshape(P, FB, KD * P))

    w1 = up(x["L0_ffn_sw1"], x["L0_ffn_rw1"], x["L0_ffn_gate_w"])
    w3 = up(x["L0_ffn_sw3"], x["L0_ffn_rw3"])
    w2 = np.zeros((P, FB, DM), f32)
    s2, r2 = x["L0_ffn_sw2"], x["L0_ffn_rw2"]
    w2[:GROW, 0] = s2[(SB - 1) * P:]
    w2[:, 1:SB] = s2[:(SB - 1) * P].reshape(SB - 1, P, DM).transpose(1, 0, 2)
    w2[:, SB:] = r2.reshape(E, RB, FE // RB, DM).transpose(0, 2, 1, 3).reshape(P, RB, DM)

    nc = bacc.Bacc("TRN2", target_bir_lowering=False, num_devices=1)
    arrays = dict(u_in=u, win_in=win, wo_in=wo, vec_in=vec, w1_in=w1, w3_in=w3, w2_in=w2)
    args = [nc.dram_tensor(name, a.shape, mybir.dt.from_np(a.dtype), kind="ExternalInput").ap()
            for name, a in arrays.items()]
    out = nc.dram_tensor("out", u.shape, F32, kind="ExternalOutput").ap()
    build(nc, *args, out)
    result = run_bass_kernel_spmd(nc, [arrays], core_ids=[0])
    return result.results[0]["out"]
```

```python
from contextlib import ExitStack

import concourse.bass as bass
from concourse import mybir

F32 = mybir.dt.float32
F32R = mybir.dt.float32r
ALU = mybir.AluOpType
ACT = mybir.ActivationFunctionType
AX = mybir.AxisListType

P = 128
DM = 256
KD = DM // P
DI = 512
H = 8
HD = DI // H
NST = 128
TAPS = 4
XBC = DI + 2 * NST
NB = XBC // P
IB, IC = 4, 5
ZH = (H + DI) // 2
ZD = 2 * ZH
WIN = ZD + XBC
KI = DI // P
TOK = 512
CH = TOK // P
SEQ = 2
EPS = 1e-5
E = 8
FE = 176
FS = 352
SB = -(-FS // P)
GROW = FS - (SB - 1) * P
RB = E * FE // P
FB = SB + RB
GROUPS = [(0, 3), (3, 7), (7, 11), (11, FB)]
V_TAP = 0
V_BIAS = V_TAP + NB * TAPS
V_NORM = V_BIAS + NB
V_DT = V_NORM + KI
V_A = V_DT + H
V_D = V_A + H
V_ALL = V_D + H


class Count:

    def __init__(self, handle, per, ahead):
        self.handle, self.per, self.ahead = handle, per, ahead


def need(eng, count, s, k):
    value = count.per * (s + 1 if count.ahead else s) + k
    if isinstance(value, int) and value <= 0:
        return
    eng.wait_ge(count.handle, value)


def need_alone(eng, count, s, k, carrier):
    need(eng, count, s, k)
    if not isinstance(s, int):
        eng.sem_inc(carrier.handle, 1)


def sig(ins, count):
    ins.then_inc(count.handle, 1)


def credit(eng, *counts):
    for c in counts:
        assert c.ahead
        eng.sem_inc(c.handle, c.per)


def product(nc, out, lh, ll, rh, rl, first, last):
    nc.tensor.matmul(out, ll, rh, start=first, stop=False)
    nc.tensor.matmul(out, lh, rl, start=False, stop=False)
    return nc.tensor.matmul(out, lh, rh, start=False, stop=last)


def flat(ap):
    return ap.rearrange("p a b -> p (a b)")


def mixer(nc, NS, u_v, win, wo, vec, x1_d):
    ctx = ExitStack()
    with ctx:
        def sb(name, shape, dt=F32):
            return ctx.enter_context(nc.sbuf_tensor(name, shape, dt))

        def sem(name, per=1, ahead=False):
            return Count(ctx.enter_context(nc.semaphore(name)), per, ahead)

        ident = sb("ident", [P, P])
        win_h = sb("win_h", [P, KD, WIN], F32R)
        win_l = sb("win_l", [P, KD, WIN], F32R)
        wo_n = sb("wo_n", [P, KI, DM])
        vecs = sb("vecs", [P, V_ALL])
        causal = sb("causal", [P, P])
        after_f = sb("after_f", [P, P])
        after = sb("after", [P, P], F32R)
        ones = sb("ones", [P, P])
        neg_half = sb("neg_half", [P, CH])
        exp_a = sb("exp_a", [P, H])
        u_ln = sb("u_ln", [P, CH, DM])
        bst = sb("bst", [P, CH, 6])
        mv = sb("mv", [P, CH, 2])
        ve = sb("ve", [P, CH])
        rstd = sb("rstd", [P, CH])
        xn = sb("xn", [P, CH, DM])
        xnt_h = sb("xnt_h", [P, KD, TOK], F32R)
        xnt_l = sb("xnt_l", [P, KD, TOK], F32R)
        sz = sb("sz", [P, 2, CH, DI])
        dt_raw = sb("dt_raw", [P, CH, H])
        raw = sb("raw", [P, 2, TAPS - 1 + TOK])
        halo = sb("halo", [P, NB, TAPS - 1])
        acc = sb("acc", [P, 2, TOK])
        xs = sb("xs", [P, 2, NB, TOK])
        v_dt = sb("v_dt", [P, CH, H])
        pos = sb("pos", [P, CH, H])
        nab = sb("nab", [P, CH, H])
        ex = sb("ex", [P, CH, H])
        den = sb("den", [P, CH, H])
        rcp = sb("rcp", [P, CH, H])
        ratio = sb("ratio", [P, CH, H])
        ratio2 = sb("ratio2", [P, CH, H])
        poly = sb("poly", [P, 2, CH, H])
        half_log = sb("half_log", [P, CH, H])
        dt = sb("dt", [P, 2, CH, H])
        a_f = sb("a_f", [P, CH, H])
        a_h = sb("a_h", [P, CH, H], F32R)
        a_l = sb("a_l", [P, CH, H], F32R)
        ecs = sb("ecs", [P, 2, 2, CH, H])
        v = sb("v", [P, CH, 2, H, P], F32R)
        decay = sb("decay", [P, CH, H, P])
        bt = sb("bt", [P, 2, NST])
        cbm = sb("cbm", [P, P])
        mix = sb("mix", [P, 2, H, P])
        xdt = sb("xdt", [P, 2, DI])
        xd = sb("xd", [P, 2, DI])
        xcd = sb("xcd", [P, DI])
        st = sb("st", [P, DI])
        st_dec = sb("st_dec", [P, DI])
        y = sb("y", [P, 2, DI])
        squares = sb("squares", [P, DI])
        ssq = sb("ssq", [P, CH])
        mse = sb("mse", [P, CH])
        rms = sb("rms", [P, CH])
        yt = sb("yt", [P, 2, KI, P])
        u_res = sb("u_res", [P, 2, CH, DM])
        x1 = sb("x1", [P, 2, CH, DM])
        stage = decay[:, :, :, :].rearrange("p a b c -> p (a b c)")
        win_f = stage[:, 0:KD * WIN].rearrange("p (k n) -> p k n", k=KD)
        wo_f = stage[:, KD * WIN:KD * WIN + KI * DM].rearrange("p (k n) -> p k n", k=KI)

        bank = [ctx.enter_context(nc.psum_tensor(f"bank{i}", [P, 512], F32)) for i in range(8)]

        vec_in = sem("vec_in")
        win_in = sem("win_in")
        wo_in = sem("wo_in")
        const_step = sem("const_step")
        carrier = sem("carrier")
        consts = sem("consts")
        exp_a_ready = sem("exp_a_ready")
        wo_ready = sem("wo_ready")
        wh_ready = sem("wh_ready")
        wl_ready = sem("wl_ready")
        u_loaded = sem("u_loaded", 16)
        stats_ready = sem("stats_ready", CH)
        mv_ready = sem("mv_ready", CH)
        ve_ready = sem("ve_ready")
        rstd_ready = sem("rstd_ready")
        xn_ready = sem("xn_ready", CH)
        xnt_ps = sem("xnt_ps", KD)
        xnth_ready = sem("xnth_ready", KD)
        xntl_ready = sem("xntl_ready", KD)
        z_ps = sem("z_ps", 2 * CH)
        dt_copied = sem("dt_copied", CH)
        z_ready = sem("z_ready", 2 * CH)
        b_ps = sem("b_ps", NB)
        raw_ready = sem("raw_ready", NB)
        acc_ready = sem("acc_ready", NB)
        halo_in = sem("halo_in", NB)
        halo_out = sem("halo_out", NB, ahead=True)
        conv_step = sem("conv_step", 3 * NB, ahead=True)
        xs_ready = sem("xs_ready", NB)
        DT_NAB, DT_A, DT_ALL = 3, 17, 19
        dt_step = sem("dt_step", DT_ALL)
        ex_ready = sem("ex_ready")
        cs_ps = sem("cs_ps")
        ecs_ready = sem("ecs_ready")
        v_ready = sem("v_ready", 2 * CH)
        seg_ps = sem("seg_ps", 2 * CH)
        decay_ready = sem("decay_ready", 2 * CH)
        cb_ps = sem("cb_ps", CH)
        bt_ready = sem("bt_ready", CH, ahead=True)
        cbm_ready = sem("cbm_ready", CH, ahead=True)
        x_ps = sem("x_ps", CH)
        xdt_ready = sem("xdt_ready", CH)
        xd_ready = sem("xd_ready", CH, ahead=True)
        mix_ready = sem("mix_ready", CH)
        xcd_ready = sem("xcd_ready", CH)
        yo_ps = sem("yo_ps", CH)
        yd_ps = sem("yd_ps", CH)
        sp_ps = sem("sp_ps", CH)
        st_decayed = sem("st_decayed", CH)
        st_ready = sem("st_ready", CH, ahead=True)
        y_off = sem("y_off", CH)
        y_sum = sem("y_sum", CH, ahead=True)
        y_skip = sem("y_skip", CH)
        y_gated = sem("y_gated", CH)
        ssq_ready = sem("ssq_ready", CH)
        mse_ready = sem("mse_ready", CH)
        rms_ready = sem("rms_ready", CH)
        yt_ps = sem("yt_ps", CH)
        yt_ready = sem("yt_ready", CH)
        op_ps = sem("op_ps", CH)
        x1_ready = sem("x1_ready", CH, ahead=True)
        res_loaded = [sem("res_loaded0"), sem("res_loaded1")]
        x1_stored = [sem("x1_stored0"), sem("x1_stored1")]

        ORDER = {
            "PE": "A0 X0 Y0 Z0 A1 Z1 Z2 Z3 B0 Y1 T0 A2 B1 O0 B2 Y2 T1 A3 B3 B4 O1 B5 Y3 S0 T2 O2 "
                  "E0 S1 T3 S2 O3 S3",
            "ACT": "A0 X0 Z0 A1 Z1 Z2 Z3 D0 A2 B0 T0 B1 B2 T1 A3 B3 B4 B5 T2 C0 S0 E0 S1 T3 S2 S3",
            "DVE": "A0 X0 L0 Y0 A1 T0 D0 Y1 A2 B0 O0 B1 T1 Y2 B2 A3 B3 B4 O1 T2 B5 Y3 O2 T3 O3 N0",
            "POOL": "A0 Y0 L0 W0 Y1 A1 B0 T0 V0 V1 B1 W1 A2 Y2 B2 V2 V3 V4 B3 Y3 T1 A3 B4 W2 V5 B5 "
                   "V6 V7 T2 W3 T3",
        }
        FRONT = "X0 Z0 Z1 Z2 Z3 D0 B0 B1 B2 B3 B4 B5 C0 V0 V1 V2 V3 V4 V5 V6 V7 S0 E0 S1 S2 S3 L0 N0"

        def step(piece, order, i, par, left):
            for name in order.split():
                if left >= (1 if name[0] in "XZDBCEVS" else 2 if name[0] in "LN" else 0):
                    piece(name[0], int(name[1]), i, par, left)

        def run(eng, name, piece):
            step(piece, FRONT, -1, 1, 2)
            with eng.Fori(0, NS // 2 - 1) as i:
                for par in range(2):
                    step(piece, ORDER[name], i, par, 2)
            for par in range(2):
                step(piece, ORDER[name], NS // 2 - 1, par, 1 - par)

        block = ctx.enter_context(nc.Block())

        @block.sync
        def _(sp):
            def load_ln(n):
                need(sp, xn_ready, n - 1, CH)
                sp.dma_start(u_ln[:, :, :], u_v[n]).then_inc(u_loaded.handle, 16)

            def load_res(i, par):
                need(sp, x1_ready, 2 * i + par - 2, CH)
                sp.dma_start(u_res[:, par], u_v[2 * i + par]).then_inc(res_loaded[par].handle, 16)

            def store_x1(i, par):
                need(sp, x1_ready, 2 * i + par, CH)
                sp.dma_start(x1_d[2 * i + par], x1[:, par]).then_inc(x1_stored[par].handle, 16)

            load_ln(0)
            sp.dma_start(vecs[:, :], vec).then_inc(vec_in.handle, 16)
            for k in range(KD):
                sp.dma_start(win_f[:, k, :], win[:, k, :]).then_inc(win_in.handle, 16)
            sp.dma_start(wo_f, wo).then_inc(wo_in.handle, 16)
            load_res(0, 0)
            load_res(0, 1)
            load_ln(1)
            with sp.Fori(0, NS // 2 - 1) as i:
                for par in range(2):
                    load_ln(2 * i + par + 2)
                    store_x1(i, par)
                    load_res(i + 1, par)
            for par in range(2):
                store_x1(NS // 2 - 1, par)
            for par in range(2):
                sp.wait_ge(x1_stored[par].handle, 16 * (NS // 2 + 1))

        @block.tensor
        def _(pe):
            def piece(kind, j, i, par, left):
                s = 2 * i + par
                n = s + 1
                tok = slice(j * P, (j + 1) * P)
                before = (s, j) if j else (s - 1, CH)
                if kind == "X":
                    for k in range(KD):
                        if k == 0:
                            need(pe, cbm_ready, s, 1)
                            need(pe, bt_ready, s, 1)
                        else:
                            need(pe, xd_ready, s, 1)
                        for c in range(CH):
                            if k == 0:
                                need(pe, xn_ready, n, c + 1)
                            last = nc.tensor.transpose(bank[2 + k][:, c * P:(c + 1) * P],
                                                       xn[:, c, k * P:(k + 1) * P], ident[:, :])
                        sig(last, xnt_ps)
                elif kind == "E":
                    need(pe, y_off, s, CH)
                    need(pe, dt_step, n, DT_A)
                    for k, mask in enumerate((ones, causal)):
                        last = nc.tensor.matmul(bank[4][:, k * CH * H:(k + 1) * CH * H], mask[:, :],
                                                flat(a_f[:, :, :]), start=True, stop=True)
                    sig(last, cs_ps)
                elif kind == "S":
                    need(pe, v_ready, n, 2 * j + 2)
                    for g in range(2):
                        if j == 0:
                            need(pe, acc_ready, n, NB - 1 + g)
                        else:
                            need(pe, decay_ready, n, 2 * (j - 1) + g + 1)
                        hs = slice(g * H // 2, (g + 1) * H // 2)
                        nc.tensor.matmul(bank[g][:, :], after[:, :], flat(v[:, j, 0, hs]),
                                         start=True, stop=False)
                        sig(nc.tensor.matmul(bank[g][:, :], after[:, :], flat(v[:, j, 1, hs]),
                                             start=False, stop=True), seg_ps)
                elif kind == "Z":
                    if j == 0:
                        need(pe, xnth_ready, n, KD)
                        need(pe, xntl_ready, n, KD)
                    for g in range(2):
                        if j == 0:
                            need(pe, decay_ready, s, 2 * CH - 1 + g)
                        else:
                            need(pe, z_ready, n, 2 * (j - 1) + g + 1)
                        cols = slice(g * ZH, (g + 1) * ZH)
                        for k in range(KD):
                            last = product(nc, bank[g][:, 0:ZH], xnt_h[:, k, tok], xnt_l[:, k, tok],
                                           win_h[:, k, cols], win_l[:, k, cols], k == 0, k == KD - 1)
                        sig(last, z_ps)
                elif kind == "B":
                    g = j % 2
                    if j < 2:
                        need(pe, z_ready, n, 2 * (CH - 1) + g + 1)
                    else:
                        need(pe, acc_ready, n, j - 1)
                    cols = slice(ZD + j * P, ZD + (j + 1) * P)
                    for k in range(KD):
                        last = product(nc, bank[g][:, :], win_h[:, k, cols], win_l[:, k, cols],
                                       xnt_h[:, k, :], xnt_l[:, k, :], k == 0, k == KD - 1)
                    sig(last, b_ps)
                elif kind == "A":
                    if j == 0:
                        need(pe, xs_ready, s, NB)
                    normalised_between = j == 1 and left >= 1
                    if normalised_between:
                        need(pe, xntl_ready, n, KD)
                    else:
                        need(pe, cbm_ready, *before)
                        need(pe, bt_ready, *before)
                    nc.tensor.matmul(bank[2][:, 0:P], xs[:, par, IB, tok], xs[:, par, IC, tok],
                                     start=True, stop=True)
                    sig(nc.tensor.transpose(bank[2][:, P:2 * P], xs[:, par, IB, tok], ident[:, :]),
                        cb_ps)
                    if not normalised_between:
                        need(pe, xd_ready, *before)
                    for b in range(KI):
                        last = nc.tensor.transpose(bank[3][:, b * P:(b + 1) * P],
                                                   xs[:, par, b, tok], ident[:, :])
                    sig(last, x_ps)
                elif kind == "Y":
                    if j == 0:
                        need(pe, ecs_ready, s, 1)
                    else:
                        need(pe, y_off, s, j)
                    need(pe, st_ready, *before)
                    sig(nc.tensor.matmul(bank[4][:, :], xs[:, par, IC, tok], st[:, :],
                                         start=True, stop=True), yo_ps)
                    need(pe, bt_ready, s, j + 1)
                    need(pe, xcd_ready, s, j + 1)
                    sig(nc.tensor.matmul(bank[6][:, :], bt[:, j % 2, :], xcd[:, :],
                                         start=True, stop=True), sp_ps)
                    need(pe, mix_ready, s, j + 1)
                    need(pe, xdt_ready, s, j + 1)
                    need(pe, y_sum, *before)
                    for h in range(H):
                        cols = slice(h * HD, min((h + 2) * HD, DI))
                        last = nc.tensor.matmul(bank[5][:, cols], mix[:, j % 2, h, :],
                                                xdt[:, j % 2, cols], start=True, stop=True)
                    sig(last, yd_ps)
                elif kind == "T":
                    need(pe, y_gated, s, j + 1)
                    need(pe, x1_ready, *before)
                    for b in range(KI):
                        last = nc.tensor.transpose(bank[7][:, b * P:(b + 1) * P],
                                                   y[:, j % 2, b * P:(b + 1) * P], ident[:, :])
                    sig(last, yt_ps)
                elif kind == "O":
                    if j == 0:
                        pe.wait_ge(wo_ready.handle, KI)
                    need(pe, yt_ready, s, j + 1)
                    for b in range(KI):
                        last = nc.tensor.matmul(bank[7][:, 0:DM], yt[:, j % 2, b, :], wo_n[:, b, :],
                                                start=b == 0, stop=b == KI - 1)
                    sig(last, op_ps)

            pe.wait_ge(consts.handle, 3)
            pe.wait_ge(wh_ready.handle, 1)
            pe.wait_ge(wl_ready.handle, 1)
            run(pe, "PE", piece)

        @block.scalar
        def _(act):
            A = nc.scalar.activation

            def silu(n, npar, b):
                need(act, conv_step, n, 3 * (b + 1))
                sig(A(xs[:, npar, b, :], acc[:, b % 2, :], ACT.Silu), xs_ready)

            def piece(kind, j, i, par, left):
                s = 2 * i + par
                n, npar = s + 1, 1 - par
                if kind == "X":
                    for k in range(KD):
                        need(act, xnt_ps, n, k + 1)
                        sig(A(xnt_h[:, k, :], bank[2 + k][:, :], ACT.Copy), xnth_ready)
                elif kind == "D":
                    need(act, dt_step, n, DT_NAB)
                    sig(A(ex[:, :, :], nab[:, :, :], ACT.Exp), ex_ready)
                elif kind == "E":
                    need(act, cs_ps, n, 1)
                    sig(A(ecs[:, npar].rearrange("p a c h -> p (a c h)"), bank[4][:, 0:2 * CH * H],
                          ACT.Exp), ecs_ready)
                elif kind == "S":
                    for g in range(2):
                        need(act, seg_ps, n, 2 * j + g + 1)
                        sig(A(flat(decay[:, j, g * H // 2:(g + 1) * H // 2]), bank[g][:, :], ACT.Exp),
                            decay_ready)
                elif kind == "Z":
                    need(act, z_ps, n, 2 * j + 1)
                    sig(A(dt_raw[:, j, :], bank[0][:, 0:H], ACT.Copy), dt_copied)
                    sig(A(sz[:, npar, j, 0:ZH - H], bank[0][:, H:ZH], ACT.Silu), z_ready)
                    need(act, z_ps, n, 2 * j + 2)
                    sig(A(sz[:, npar, j, ZH - H:DI], bank[1][:, 0:ZH], ACT.Silu), z_ready)
                elif kind == "B":
                    g = j % 2
                    if j >= 2:
                        need(act, conv_step, n, 3 * (j - 1))
                        need(act, halo_out, n, j - 1)
                        need(act, xs_ready, n, j - 1)
                    else:
                        need(act, conv_step, n - 1, 3 * (NB - 1 + j))
                        need(act, halo_out, n - 1, NB - 1 + j)
                        need(act, xs_ready, n - 1, NB - 1 + j)
                    need(act, b_ps, n, j + 1)
                    sig(A(raw[:, g, TAPS - 1:], bank[g][:, :], ACT.Copy), raw_ready)
                    tap = V_TAP + j * TAPS + TAPS - 1
                    sig(A(acc[:, g, :], bank[g][:, :], ACT.Identity, bias=vecs[:, V_BIAS + j:V_BIAS + j + 1],
                          scale=vecs[:, tap:tap + 1]), acc_ready)
                    if j:
                        silu(n, npar, j - 1)
                elif kind == "C":
                    silu(n, npar, NB - 1)
                elif kind == "A":
                    need(act, cb_ps, s, j + 1)
                    sig(A(bt[:, j % 2, :], bank[2][:, P:2 * P], ACT.Copy), bt_ready)
                elif kind == "T":
                    need(act, y_gated, s, j + 1)
                    sig(A(squares[:, :], y[:, j % 2, :], ACT.Square, accum_out=ssq[:, j:j + 1]),
                        ssq_ready)
                    need(act, yt_ps, s, j + 1)
                    sig(A(flat(yt[:, j % 2]), bank[7][:, :], ACT.Copy), yt_ready)

            credit(act, bt_ready)
            act.wait_ge(win_in.handle, 16 * KD)
            A(win_h[:, :, :], win_f, ACT.Copy).then_inc(wh_ready.handle, 1)
            act.wait_ge(vec_in.handle, 16)
            A(exp_a[:, :], vecs[:, V_A:V_A + H], ACT.Exp).then_inc(exp_a_ready.handle, 1)
            run(act, "ACT", piece)

        @block.vector
        def _(dve):
            V = nc.vector

            def statistics(n):
                need(dve, u_loaded, n, 16)
                for c in range(CH):
                    sig(V.bn_stats(bst[:, c, :], u_ln[:, c, :]), stats_ready)
                for c in range(CH):
                    need_alone(dve, stats_ready, n, c + 1, carrier)
                    sig(V.bn_aggr(mv[:, c, :], bst[:, c, :]), mv_ready)

            def normalise(n):
                need(dve, rstd_ready, n, 1)
                need(dve, xnt_ps, n - 1, KD)
                for c in range(CH):
                    sig(V.tensor_scalar(xn[:, c, :], u_ln[:, c, :], mv[:, c, 0:1], rstd[:, c:c + 1],
                                        ALU.subtract, ALU.mult), xn_ready)

            def step_sizes(n, npar):
                done = [0]

                def link(ins):
                    sig(ins, dt_step)
                    done[0] += 1
                    need(dve, dt_step, n, done[0])

                over_chunks = lambda ap: ap.unsqueeze(1).to_broadcast([P, CH, H])
                need(dve, dt_copied, n, CH)
                link(V.tensor_tensor(v_dt[:, :, :], dt_raw[:, :, :], over_chunks(vecs[:, V_DT:V_DT + H]),
                                     ALU.add))
                link(V.tensor_scalar(pos[:, :, :], v_dt[:, :, :], 0.0, None, ALU.max))
                link(V.scalar_tensor_tensor(nab[:, :, :], v_dt[:, :, :], -1.0, v_dt[:, :, :],
                                            ALU.mult, ALU.min))
                assert done[0] == DT_NAB
                need(dve, ex_ready, n, 1)
                link(V.tensor_scalar(den[:, :, :], ex[:, :, :], 2.0, None, ALU.add))
                link(V.reciprocal(rcp[:, :, :], den[:, :, :]))
                link(V.tensor_tensor(ratio[:, :, :], ex[:, :, :], rcp[:, :, :], ALU.mult))
                link(V.tensor_tensor(ratio2[:, :, :], ratio[:, :, :], ratio[:, :, :], ALU.mult))
                link(V.tensor_scalar(poly[:, 0], ratio2[:, :, :], 1.0 / 15, None, ALU.mult))
                for k, odd in enumerate((13, 11, 9, 7, 5, 3)):
                    link(V.scalar_tensor_tensor(poly[:, (k + 1) % 2], poly[:, k % 2], 1.0 / odd,
                                                ratio2[:, :, :], ALU.add, ALU.mult))
                link(V.scalar_tensor_tensor(half_log[:, :, :], poly[:, 0], 1.0, ratio[:, :, :],
                                            ALU.add, ALU.mult))
                link(V.scalar_tensor_tensor(dt[:, npar], half_log[:, :, :], 2.0, pos[:, :, :],
                                            ALU.mult, ALU.add))
                need(dve, cs_ps, n - 1, 1)
                need(dve, v_ready, n - 1, 2 * CH)
                link(V.scalar_tensor_tensor(a_f[:, :, :], dt[:, npar], -1.0, over_chunks(exp_a[:, :]),
                                            ALU.mult, ALU.mult))
                assert done[0] == DT_A
                link(V.tensor_copy(a_h[:, :, :], a_f[:, :, :]))
                link(V.tensor_tensor(a_l[:, :, :], a_f[:, :, :], a_h[:, :, :].bitcast(F32), ALU.subtract))
                assert done[0] == DT_ALL

            def heads(ap):
                return ap.rearrange("p (h d) -> p h d", h=H)

            def per_head(ap):
                return ap.unsqueeze(2).to_broadcast([P, H, HD])

            def piece(kind, j, i, par, left):
                s = 2 * i + par
                n = s + 1
                if kind == "X":
                    for k in range(KD):
                        need(dve, xnth_ready, n, k + 1)
                        sig(V.tensor_tensor(xnt_l[:, k, :], bank[2 + k][:, :],
                                            xnt_h[:, k, :].bitcast(F32), ALU.subtract), xntl_ready)
                elif kind == "L":
                    statistics(s + 2)
                elif kind == "N":
                    normalise(s + 2)
                elif kind == "D":
                    step_sizes(n, 1 - par)
                elif kind == "B":
                    g = j % 2
                    need(dve, raw_ready, n, j + 1)
                    need(dve, halo_in, n, j + 1)
                    need(dve, acc_ready, n, j + 1)
                    for t in range(TAPS - 1):
                        if t:
                            need(dve, conv_step, n, 3 * j + t)
                        tap = V_TAP + j * TAPS + t
                        sig(V.scalar_tensor_tensor(acc[:, g, :], raw[:, g, t:t + TOK],
                                                   vecs[:, tap:tap + 1], acc[:, g, :],
                                                   ALU.mult, ALU.add), conv_step)
                elif kind == "A":
                    need(dve, bt_ready, s, j + 1)
                    sig(V.tensor_tensor(cbm[:, :], bank[2][:, 0:P], causal[:, :], ALU.mult), cbm_ready)
                    need(dve, x_ps, s, j + 1)
                    sig(V.tensor_tensor(heads(xdt[:, j % 2, :]), heads(bank[3][:, :]),
                                        per_head(dt[:, par, j, :]), ALU.mult), xdt_ready)
                    sig(V.tensor_tensor(heads(xd[:, j % 2, :]), heads(bank[3][:, :]),
                                        per_head(vecs[:, V_D:V_D + H]), ALU.mult), xd_ready)
                    need(dve, cbm_ready, s, j + 1)
                    need(dve, decay_ready, s, 2 * j + 2)
                    sig(V.tensor_tensor(mix[:, j % 2], decay[:, j],
                                        cbm[:, :].unsqueeze(1).to_broadcast([P, H, P]), ALU.mult),
                        mix_ready)
                elif kind == "Y":
                    need(dve, ecs_ready, s, 1)
                    need(dve, yo_ps, s, j + 1)
                    sig(V.tensor_tensor(heads(y[:, j % 2, :]), heads(bank[4][:, :]),
                                        per_head(ecs[:, par, 1, j, :]), ALU.mult), y_off)
                    need(dve, st_decayed, s, j + 1)
                    need(dve, sp_ps, s, j + 1)
                    if par == SEQ - 1 and j == CH - 1:
                        sig(V.memset(st[:, :], 0.0), st_ready)
                    else:
                        sig(V.tensor_tensor(st[:, :], st_dec[:, :], bank[6][:, :], ALU.add), st_ready)
                    need(dve, y_off, s, j + 1)
                    need(dve, yd_ps, s, j + 1)
                    sig(V.tensor_tensor(y[:, j % 2, :], y[:, j % 2, :], bank[5][:, :], ALU.add), y_sum)
                elif kind == "T":
                    need(dve, y_skip, s, j + 1)
                    sig(V.tensor_tensor(y[:, j % 2, :], y[:, j % 2, :], sz[:, par, j, :], ALU.mult),
                        y_gated)
                elif kind == "O":
                    if j == 0:
                        dve.wait_ge(res_loaded[par].handle, 16 * (i + 1))
                        dve.wait_ge(x1_stored[par].handle, 16 * (i + 1))
                    need(dve, rms_ready, s, j + 1)
                    need(dve, op_ps, s, j + 1)
                    sig(V.scalar_tensor_tensor(x1[:, par, j, :], bank[7][:, 0:DM], rms[:, j:j + 1],
                                               u_res[:, par, j, :], ALU.mult, ALU.add), x1_ready)

            credit(dve, conv_step, cbm_ready, xd_ready, st_ready, y_sum, x1_ready)
            for par in range(2):
                dve.sem_inc(x1_stored[par].handle, 16)
            V.memset(st[:, :], 0.0).then_inc(consts.handle, 1)
            statistics(0)
            normalise(0)
            dve.wait_ge(wh_ready.handle, 1)
            V.tensor_tensor(win_l[:, :, :], win_f, win_h[:, :, :].bitcast(F32), ALU.subtract)\
                .then_inc(wl_ready.handle, 1)
            dve.wait_ge(vec_in.handle, 16)
            dve.wait_ge(wo_in.handle, 16)
            for b in range(KI):
                V.tensor_scalar(wo_n[:, b, :], wo_f[:, b, :], vecs[:, V_NORM + b:V_NORM + b + 1], None,
                                ALU.mult).then_inc(wo_ready.handle, 1)
            dve.wait_ge(exp_a_ready.handle, 1)
            dve.wait_ge(consts.handle, 3)
            run(dve, "DVE", piece)

        @block.gpsimd
        def _(pool):
            G = nc.gpsimd

            def rstd_of(n):
                need_alone(pool, mv_ready, n, CH, carrier)
                sig(G.tensor_scalar(ve[:, :], mv[:, :, 1], EPS, None, ALU.add), ve_ready)
                need(pool, ve_ready, n, 1)
                sig(G.tensor_tensor(rstd[:, :], ve[:, :], neg_half[:, :], ALU.pow), rstd_ready)

            def piece(kind, j, i, par, left):
                s = 2 * i + par
                n, npar = s + 1, 1 - par
                if kind == "V":
                    need(pool, dt_step, n, DT_ALL)
                    c, src = j // 2, (a_h, a_l)[j % 2]
                    need(pool, seg_ps, n - 1, 2 * c + 2)
                    sig(G.tensor_tensor(v[:, c, j % 2], causal[:, :].unsqueeze(1).to_broadcast([P, H, P]),
                                        src[:, c, :].bitcast(F32).unsqueeze(2).to_broadcast([P, H, P]),
                                        ALU.mult), v_ready)
                elif kind == "L":
                    rstd_of(s + 2)
                elif kind == "B":
                    g = j % 2
                    need_alone(pool, conv_step,
                               *((n, 3 * (j - 1)) if j >= 2 else (n - 1, 3 * (NB - 1 + j))), carrier)
                    if npar == 0:
                        sig(G.memset(raw[:, g, 0:TAPS - 1], 0.0), halo_in)
                    else:
                        need_alone(pool, halo_out, n - 1, j + 1, carrier)
                        sig(G.tensor_copy(raw[:, g, 0:TAPS - 1], halo[:, j, :]), halo_in)
                    need(pool, halo_in, n, j + 1)
                    need_alone(pool, raw_ready, n, j + 1, carrier)
                    sig(G.tensor_copy(halo[:, j, :], raw[:, g, TOK:TOK + TAPS - 1]), halo_out)
                elif kind == "A":
                    need(pool, xdt_ready, s, j + 1)
                    need(pool, decay_ready, s, 2 * j + 2)
                    sig(G.tensor_tensor(xcd[:, :].rearrange("p (h d) -> p h d", h=H),
                                        xdt[:, j % 2, :].rearrange("p (h d) -> p h d", h=H),
                                        decay[:, j, :, P - 1:P].to_broadcast([P, H, HD]), ALU.mult),
                        xcd_ready)
                elif kind == "Y":
                    need(pool, ecs_ready, s, 1)
                    need(pool, st_ready, *((s, j) if j else (s - 1, CH)))
                    sig(G.tensor_tensor(st_dec[:, :].rearrange("p (h d) -> p h d", h=H),
                                        st[:, :].rearrange("p (h d) -> p h d", h=H),
                                        ecs[:, par, 0, j, :].unsqueeze(2).to_broadcast([P, H, HD]),
                                        ALU.mult), st_decayed)
                elif kind == "W":
                    need(pool, y_sum, s, j + 1)
                    sig(G.tensor_tensor(y[:, j % 2, :], y[:, j % 2, :], xd[:, j % 2, :], ALU.add), y_skip)
                elif kind == "T":
                    need_alone(pool, ssq_ready, s, j + 1, carrier)
                    sig(G.tensor_scalar(mse[:, j:j + 1], ssq[:, j:j + 1], 1.0 / DI, EPS,
                                        ALU.mult, ALU.add), mse_ready)
                    need(pool, mse_ready, s, j + 1)
                    sig(G.tensor_tensor(rms[:, j:j + 1], mse[:, j:j + 1], neg_half[:, 0:1], ALU.pow),
                        rms_ready)

            credit(pool, halo_out)
            for m, value in ((ident, 0.0), (causal, 1.0), (after_f, 1.0), (ones, 1.0), (neg_half, -0.5)):
                G.memset(m[:, :], value).then_inc(const_step.handle, 1)
            pool.wait_ge(const_step.handle, 5)
            for m, op, fill, a, b in ((ident, ALU.not_equal, 1.0, -1, 1), (causal, ALU.is_ge, 0.0, 1, -1),
                                      (after_f, ALU.is_gt, 0.0, -1, 1)):
                G.affine_select(out=m[:, :], in_=m[:, :], compare_op=op, fill=fill, base=0,
                                pattern=[[a, P]], channel_multiplier=b).then_inc(const_step.handle, 1)
            pool.wait_ge(const_step.handle, 8)
            G.tensor_copy(after[:, :], after_f[:, :]).then_inc(const_step.handle, 1)
            pool.wait_ge(const_step.handle, 9)
            G.memset(halo[:, :, :], 0.0).then_inc(consts.handle, 2)
            rstd_of(0)
            run(pool, "POOL", piece)


def experts(nc, NS, x1_d, w1, w3, w2, out_v):
    ctx = ExitStack()
    with ctx:
        def sb(name, shape, dt=F32):
            return ctx.enter_context(nc.sbuf_tensor(name, shape, dt))

        def sem(name, per=1, ahead=False):
            return Count(ctx.enter_context(nc.semaphore(name)), per, ahead)

        w1_f = sb("w1_f", [P, FB, KD * P])
        w3_f = sb("w3_f", [P, FB, KD * P])
        w2_f = sb("w2_f", [P, FB, DM])
        w1_h = sb("w1_h", [P, FB, KD * P], F32R)
        w1_l = sb("w1_l", [P, FB, KD * P], F32R)
        w3_h = sb("w3_h", [P, FB, KD * P], F32R)
        w3_l = sb("w3_l", [P, FB, KD * P], F32R)
        w2_h = sb("w2_h", [P, FB, DM], F32R)
        w2_l = sb("w2_l", [P, FB, DM], F32R)
        ident = sb("ident2", [P, P])
        sel_f = sb("sel_f", [2 * E, 2, P])
        sel = sb("sel", [2 * E, P], F32R)
        neg_half = sb("neg_half2", [P, CH])
        rank = sb("rank", [P, E])
        x1 = sb("x1_in", [P, 2, CH, DM])
        bst = sb("bst2", [P, CH, 6])
        mv = sb("mv2", [P, CH, 2])
        ve = sb("ve2", [P, CH])
        rstd = sb("rstd2", [P, CH])
        xn = sb("xn2", [P, CH, DM])
        xt_h = sb("xt_h", [P, 2, KD, TOK], F32R)
        xt_l = sb("xt_l", [P, 2, KD, TOK], F32R)
        lg = sb("lg", [P, TOK])
        lgt = sb("lgt", [P, CH, E])
        shifted = sb("shifted", [P, CH, E])
        ep = sb("ep", [P, CH, E])
        score = sb("score", [P, CH, E])
        top = sb("top", [P, CH])
        total = sb("total", [P, CH])
        inv = sb("inv", [P, CH])
        tied = sb("tied", [P, CH, E])
        tied_rank = sb("tied_rank", [P, CH, E])
        best_rank = sb("best_rank", [P, CH])
        pick1 = sb("pick1", [P, CH, E])
        pick2 = sb("pick2", [P, CH, E])
        rest = sb("rest", [P, CH, E])
        cw = sb("cw", [P, CH, E])
        cw_r = sb("cw_r", [P, CH, E], F32R)
        cw_parts = sb("cw_parts", [P, CH, 2 * E])
        cwt = sb("cwt", [2 * E, TOK], F32R)
        cwb = sb("cwb", [P, TOK])
        act1 = sb("act1", [P, 2, TOK])
        g = sb("g", [P, 2, TOK])
        g_h = sb("g_h", [P, 2, TOK], F32R)
        g_l = sb("g_l", [P, 2, TOK], F32R)
        y2t = sb("y2t", [P, KD, TOK])
        ob = sb("ob", [P, CH, DM])
        bank = [ctx.enter_context(nc.psum_tensor(f"ebank{k}", [P, 512], F32)) for k in range(8)]

        w_in = [sem(f"w_in{k}") for k in range(len(GROUPS))]
        wh_ready = sem("e_wh_ready")
        wl_ready = sem("e_wl_ready")
        const_step = sem("e_const_step")
        carrier = sem("e_carrier")
        consts = sem("e_consts")
        x1_loaded = [sem("x1_loaded0"), sem("x1_loaded1")]
        stats_ready = sem("e_stats_ready", CH)
        mv_ready = sem("e_mv_ready", CH)
        ve_ready = sem("e_ve_ready")
        rstd_ready = sem("e_rstd_ready")
        xn_ready = sem("e_xn_ready", CH)
        xt_ps = sem("xt_ps", KD)
        xth_ready = sem("xth_ready", KD)
        xtl_ready = sem("xtl_ready", KD)
        h1_ps = sem("h1_ps", FB)
        h3_ps = sem("h3_ps", FB)
        act_ready = sem("act_ready", FB)
        lg_ready = sem("lg_ready")
        lg_ps = sem("lg_ps")
        lgt_ready = sem("lgt_ready")
        R_SHIFT, R_ALL = 2, 21
        route = sem("route", R_ALL)
        ep_ready = sem("ep_ready")
        cwt_ps = sem("cwt_ps")
        cwt_ready = sem("cwt_ready")
        cwb_ps = sem("cwb_ps")
        cwb_ready = sem("cwb_ready")
        prod_ready = sem("prod_ready", FB)
        g_ready = sem("g_ready", RB)
        gh_ready = sem("gh_ready", FB)
        gl_ready = sem("gl_ready", FB)
        down_ps = sem("down_ps", FB)
        y2_ready = sem("y2_ready", KD)
        ot_ps = sem("ot_ps", 2)
        ob_ready = sem("ob_ready", 2)
        stored = sem("stored", 16, ahead=True)

        ORDER = ["F0", "H0", f"D{FB - 1}", "K0", "G0", "F1", "H1", "D0", "Q0", "F2", "H2", "D1",
                 "C0", "F3", "S0", "H3", "D2"]
        for j in range(4, FB):
            ORDER += [f"F{j}", f"H{j}"] + (["L0"] if j == 5 else []) + (["X0"] if j == 9 else [])
            ORDER += [f"D{j - 1}"]

        def step(piece, n, par, loads, first, last):
            for name in ORDER:
                kind, j = name[0], int(name[1:])
                before = kind in "KQ" or name == f"D{FB - 1}"
                if (before and first) or (kind in "LX" and last):
                    continue
                piece(kind, j, n - 1 if before else n, 1 - par if before else par,
                      loads if kind == "L" else None, first)

        def run(eng, piece):
            step(piece, 0, 0, 1, True, False)
            with eng.Fori(0, NS // 2 - 1) as i:
                step(piece, 2 * i + 1, 1, i + 2, False, False)
                step(piece, 2 * i + 2, 0, i + 2, False, False)
            step(piece, NS - 1, 1, None, False, True)
            for kind, j in (("D", FB - 1), ("K", 0), ("Q", 0)):
                piece(kind, j, NS - 1, 1, None, False)

        block = ctx.enter_context(nc.Block())

        @block.sync
        def _(sp):
            def load(n, par):
                need(sp, ob_ready, n - 2, 2)
                sp.dma_start(x1[:, par], x1_d[n]).then_inc(x1_loaded[par].handle, 16)

            def store(n):
                need(sp, ob_ready, n, 2)
                sp.dma_start(out_v[n], ob[:, :, :]).then_inc(stored.handle, 16)

            credit(sp, stored)
            load(0, 0)
            for k, (a, b) in enumerate(GROUPS):
                for dst, src in ((w1_f, w1), (w3_f, w3), (w2_f, w2)):
                    sp.dma_start(dst[:, a:b, :], src[:, a:b, :]).then_inc(w_in[k].handle, 16)
            load(1, 1)
            with sp.Fori(0, NS // 2 - 1) as i:
                for par in range(2):
                    store(2 * i + par)
                    load(2 * i + par + 2, par)
            store(NS - 2)
            store(NS - 1)
            need(sp, stored, NS - 1, 16)

        @block.tensor
        def _(pe):
            def transposes(n, par):
                for k in range(KD):
                    for c in range(CH):
                        if k == 0:
                            need(pe, xn_ready, n, c + 1)
                        last = nc.tensor.transpose(bank[6 + k][:, c * P:(c + 1) * P],
                                                   xn[:, c, k * P:(k + 1) * P], ident[:, :])
                    sig(last, xt_ps)

            def piece(kind, j, n, par, loads, first):
                if kind == "F":
                    b = j % 2
                    if j == 0:
                        need(pe, xth_ready, n, KD)
                        need(pe, xtl_ready, n, KD)
                    if first:
                        for k, (a, _) in enumerate(GROUPS):
                            if a == j:
                                pe.wait_ge(wh_ready.handle, 3 * (k + 1))
                                pe.wait_ge(wl_ready.handle, 3 * (k + 1))
                    need(pe, act_ready, *((n, j - 1) if j >= 2 else (n - 1, FB - 1 + j)))
                    if j == 2:
                        need(pe, lg_ready, n, 1)
                    for k in range(KD):
                        cols = slice(k * P, (k + 1) * P)
                        last = product(nc, bank[2 + b][:, :], w1_h[:, j, cols], w1_l[:, j, cols],
                                       xt_h[:, par, k, :], xt_l[:, par, k, :], k == 0, k == KD - 1)
                    sig(last, h1_ps)
                    need(pe, prod_ready, *((n, j - 1) if j >= 2 else (n - 1, FB - 1 + j)))
                    for k in range(KD):
                        cols = slice(k * P, (k + 1) * P)
                        last = product(nc, bank[4 + b][:, :], w3_h[:, j, cols], w3_l[:, j, cols],
                                       xt_h[:, par, k, :], xt_l[:, par, k, :], k == 0, k == KD - 1)
                    sig(last, h3_ps)
                elif kind == "D":
                    need(pe, gh_ready, n, j + 1)
                    need(pe, gl_ready, n, j + 1)
                    if j == 0:
                        need(pe, y2_ready, n - 1, KD)
                    for k in range(KD):
                        cols = slice(k * P, (k + 1) * P)
                        last = product(nc, bank[k][:, :], w2_h[:, j, cols], w2_l[:, j, cols],
                                       g_h[:, j % 2, :], g_l[:, j % 2, :], j == 0, j == FB - 1)
                    sig(last, down_ps)
                elif kind == "G":
                    need(pe, lg_ready, n, 1)
                    need_alone(pe, xtl_ready, n, KD, carrier)
                    for c in range(CH):
                        last = nc.tensor.transpose(bank[6][:, c * 32:(c + 1) * 32],
                                                   lg[GROW:P, c * P:(c + 1) * P], ident[GROW:P, GROW:P])
                    sig(last, lg_ps)
                elif kind == "C":
                    need(pe, route, n, R_ALL)
                    if not first:
                        need(pe, ob_ready, n - 1, 2)
                    for c in range(CH):
                        last = nc.tensor.transpose(bank[7][0:2 * E, c * P:(c + 1) * P],
                                                   cw_parts[:, c, :], ident[:, :])
                    sig(last, cwt_ps)
                elif kind == "S":
                    need(pe, cwt_ready, n, 1)
                    if not first:
                        need(pe, ob_ready, n - 1, 1)
                    need(pe, lgt_ready, n, 1)
                    sig(nc.tensor.matmul(bank[6][:, :], sel[:, :], cwt[:, :], start=True, stop=True), cwb_ps)
                elif kind == "Q":
                    need(pe, y2_ready, n, KD)
                    if isinstance(n, int) and n == NS - 1:
                        need(pe, cwb_ready, n, 1)
                    else:
                        need(pe, lgt_ready, n + 1, 1)
                    for t in range(2):
                        for c in range(2):
                            tok = slice((2 * t + c) * P, (2 * t + c + 1) * P)
                            for k in range(KD):
                                at = c * DM + k * P
                                last = nc.tensor.transpose(bank[6 + t][:, at:at + P], y2t[:, k, tok],
                                                           ident[:, :])
                        sig(last, ot_ps)
                elif kind == "X":
                    need(pe, cwb_ready, n, 1)
                    transposes(n + 1, 1 - par)

            pe.wait_ge(consts.handle, 1)
            transposes(0, 0)
            run(pe, piece)

        @block.scalar
        def _(act):
            A = nc.scalar.activation

            def split_xt(n, par):
                for k in range(KD):
                    need(act, xt_ps, n, k + 1)
                    sig(A(xt_h[:, par, k, :], bank[6 + k][:, :], ACT.Copy), xth_ready)

            def split_weights(k):
                a, b = GROUPS[k]
                act.wait_ge(w_in[k].handle, 48)
                for dst, src in ((w1_h, w1_f), (w3_h, w3_f), (w2_h, w2_f)):
                    sig(A(dst[:, a:b, :], src[:, a:b, :], ACT.Copy), wh_ready)

            def piece(kind, j, n, par, loads, first):
                if kind == "F":
                    need(act, h1_ps, n, j + 1)
                    need(act, prod_ready, *((n, j - 1) if j >= 2 else (n - 1, FB - 1 + j)))
                    sig(A(act1[:, j % 2, :], bank[2 + j % 2][:, :], ACT.Silu), act_ready)
                    if j == 0:
                        sig(A(lg[GROW:P, :], bank[2][GROW:P, :], ACT.Copy), lg_ready)
                    if first:
                        for k, (a, _) in enumerate(GROUPS):
                            if a == j + 2 and k:
                                split_weights(k)
                elif kind == "H":
                    if j < SB:
                        need(act, prod_ready, n, j + 1)
                    else:
                        need(act, g_ready, n, j - SB + 1)
                    need(act, down_ps, *((n, j - 1) if j >= 2 else (n - 1, FB - 1 + j)))
                    sig(A(g_h[:, j % 2, :], g[:, j % 2, :], ACT.Copy), gh_ready)
                elif kind == "G":
                    need(act, lg_ps, n, 1)
                    sig(A(lgt[:, :, :], bank[6][:, 0:CH * 32].rearrange("p (c e) -> p c e", c=CH)[:, :, 0:E],
                          ACT.Copy), lgt_ready)
                    need(act, route, n, R_SHIFT)
                    sig(A(ep[:, :, :], shifted[:, :, :], ACT.Exp), ep_ready)
                elif kind == "C":
                    need(act, cwt_ps, n, 1)
                    sig(A(cwt[:, :], bank[7][0:2 * E, :], ACT.Copy), cwt_ready)
                elif kind == "S":
                    need(act, cwb_ps, n, 1)
                    sig(A(cwb[:, :], bank[6][:, :], ACT.Copy), cwb_ready)
                elif kind == "K":
                    need(act, down_ps, n, FB)
                    for k in range(KD):
                        sig(A(y2t[:, k, :], bank[k][:, :], ACT.Copy), y2_ready)
                elif kind == "X":
                    split_xt(n + 1, 1 - par)

            split_weights(0)
            split_xt(0, 0)
            run(act, piece)

        @block.vector
        def _(dve):
            V = nc.vector

            def layer_norm(n, par, loads):
                dve.wait_ge(x1_loaded[par].handle, 16 * loads)
                for c in range(CH):
                    sig(V.bn_stats(bst[:, c, :], x1[:, par, c, :]), stats_ready)
                for c in range(CH):
                    need_alone(dve, stats_ready, n, c + 1, carrier)
                    sig(V.bn_aggr(mv[:, c, :], bst[:, c, :]), mv_ready)
                need(dve, rstd_ready, n, 1)
                need(dve, xt_ps, n - 1, KD)
                for c in range(CH):
                    sig(V.tensor_scalar(xn[:, c, :], x1[:, par, c, :], mv[:, c, 0:1], rstd[:, c:c + 1],
                                        ALU.subtract, ALU.mult), xn_ready)

            def split_xt(n, par):
                for k in range(KD):
                    need(dve, xth_ready, n, k + 1)
                    sig(V.tensor_tensor(xt_l[:, par, k, :], bank[6 + k][:, :],
                                        xt_h[:, par, k, :].bitcast(F32), ALU.subtract), xtl_ready)

            def split_weights(k):
                a, b = GROUPS[k]
                for m, (dst, src, hi) in enumerate(((w1_l, w1_f, w1_h), (w3_l, w3_f, w3_h),
                                                    (w2_l, w2_f, w2_h))):
                    dve.wait_ge(wh_ready.handle, 3 * k + m + 1)
                    sig(V.tensor_tensor(dst[:, a:b, :], src[:, a:b, :], hi[:, a:b, :].bitcast(F32),
                                        ALU.subtract), wl_ready)

            def routing(n):
                done = [0]

                def link(ins):
                    sig(ins, route)
                    done[0] += 1
                    need(dve, route, n, done[0])

                per_tok = lambda ap: ap.unsqueeze(2).to_broadcast([P, CH, E])
                ranks = rank[:, :].unsqueeze(1).to_broadcast([P, CH, E])
                need(dve, lgt_ready, n, 1)
                link(V.tensor_reduce(top[:, :], lgt[:, :, :], AX.X, ALU.max))
                link(V.tensor_tensor(shifted[:, :, :], lgt[:, :, :], per_tok(top[:, :]), ALU.subtract))
                assert done[0] == R_SHIFT
                need(dve, ep_ready, n, 1)
                link(V.tensor_reduce(total[:, :], ep[:, :, :], AX.X, ALU.add))
                link(V.reciprocal(inv[:, :], total[:, :]))
                link(V.tensor_tensor(score[:, :, :], ep[:, :, :], per_tok(inv[:, :]), ALU.mult))
                for left, pick in ((score, pick1), (rest, pick2)):
                    link(V.tensor_reduce(top[:, :], left[:, :, :], AX.X, ALU.max))
                    link(V.tensor_tensor(tied[:, :, :], left[:, :, :], per_tok(top[:, :]), ALU.is_equal))
                    link(V.tensor_tensor(tied_rank[:, :, :], tied[:, :, :], ranks, ALU.mult))
                    link(V.tensor_reduce(best_rank[:, :], tied_rank[:, :, :], AX.X, ALU.max))
                    link(V.tensor_tensor(pick[:, :, :], tied_rank[:, :, :], per_tok(best_rank[:, :]),
                                         ALU.is_equal))
                    if pick is pick1:
                        link(V.scalar_tensor_tensor(rest[:, :, :], pick1[:, :, :], -2.0, score[:, :, :],
                                                    ALU.mult, ALU.add))
                link(V.tensor_tensor(tied[:, :, :], pick1[:, :, :], pick2[:, :, :], ALU.add))
                link(V.tensor_tensor(cw[:, :, :], score[:, :, :], tied[:, :, :], ALU.mult))
                link(V.tensor_copy(cw_r[:, :, :], cw[:, :, :]))
                link(V.tensor_copy(cw_parts[:, :, 0:E], cw_r[:, :, :].bitcast(F32)))
                link(V.tensor_tensor(cw_parts[:, :, E:2 * E], cw[:, :, :], cw_r[:, :, :].bitcast(F32),
                                     ALU.subtract))
                assert done[0] == R_ALL

            def piece(kind, j, n, par, loads, first):
                if kind == "F":
                    need(dve, act_ready, n, j + 1)
                    need(dve, h3_ps, n, j + 1)
                    need(dve, gl_ready, *((n, j - 1) if j >= 2 else (n - 1, FB - 1 + j)))
                    sig(V.tensor_tensor(g[:, j % 2, :], bank[4 + j % 2][:, :], act1[:, j % 2, :], ALU.mult),
                        prod_ready)
                    if first:
                        for k, (a, _) in enumerate(GROUPS):
                            if a == j + 2 and k:
                                split_weights(k)
                elif kind == "G":
                    routing(n)
                elif kind == "H" and j >= SB:
                    if j == SB:
                        need(dve, cwb_ready, n, 1)
                    need(dve, prod_ready, n, j + 1)
                    sig(V.tensor_tensor(g[:, j % 2, :], g[:, j % 2, :], cwb[:, :], ALU.mult), g_ready)
                elif kind == "Q":
                    need(dve, stored, n - 1, 16)
                    for t in range(2):
                        need(dve, ot_ps, n, t + 1)
                        sig(V.tensor_tensor(flat(ob[:, 2 * t:2 * t + 2, :]), bank[6 + t][:, :],
                                            flat(x1[:, par, 2 * t:2 * t + 2, :]), ALU.add), ob_ready)
                elif kind == "L":
                    layer_norm(n + 1, 1 - par, loads)
                elif kind == "X":
                    split_xt(n + 1, 1 - par)

            layer_norm(0, 0, 1)
            split_weights(0)
            split_xt(0, 0)
            run(dve, piece)

        @block.gpsimd
        def _(pool):
            G = nc.gpsimd

            def rstd_of(n):
                need_alone(pool, mv_ready, n, CH, carrier)
                sig(G.tensor_scalar(ve[:, :], mv[:, :, 1], EPS, None, ALU.add), ve_ready)
                need(pool, ve_ready, n, 1)
                sig(G.tensor_tensor(rstd[:, :], ve[:, :], neg_half[:, :], ALU.pow), rstd_ready)

            def piece(kind, j, n, par, loads, first):
                if kind == "H":
                    need(pool, gh_ready, n, j + 1)
                    sig(G.tensor_tensor(g_l[:, j % 2, :], g[:, j % 2, :], g_h[:, j % 2, :].bitcast(F32),
                                        ALU.subtract), gl_ready)
                elif kind == "L":
                    rstd_of(n + 1)

            const = [0]

            def made(ins):
                ins.then_inc(const_step.handle, 1)
                const[0] += 1

            made(G.memset(ident[:, :], 0.0))
            made(G.memset(neg_half[:, :], -0.5))
            made(G.memset(sel_f[:, :, :], 1.0))
            for e in range(E):
                made(G.memset(rank[:, e:e + 1], float(E - e)))
            pool.wait_ge(const_step.handle, const[0])
            made(G.affine_select(out=ident[:, :], in_=ident[:, :], compare_op=ALU.not_equal, fill=1.0,
                                 base=0, pattern=[[-1, P]], channel_multiplier=1))
            wide = P // E
            for k in range(2):
                made(G.affine_select(out=sel_f[:, k, :], in_=sel_f[:, k, :], compare_op=ALU.is_ge, fill=0.0,
                                     base=k * P, pattern=[[1, P]], channel_multiplier=-wide))
            pool.wait_ge(const_step.handle, const[0])
            for k in range(2):
                made(G.affine_select(out=sel_f[:, k, :], in_=sel_f[:, k, :], compare_op=ALU.is_ge, fill=0.0,
                                     base=wide - 1 - k * P, pattern=[[-1, P]], channel_multiplier=wide))
            pool.wait_ge(const_step.handle, const[0])
            G.tensor_tensor(sel[:, :], sel_f[:, 0, :], sel_f[:, 1, :], ALU.add).then_inc(consts.handle, 1)
            rstd_of(0)
            run(pool, piece)


def build(nc, u, win, wo, vec, w1, w3, w2, out):
    NS = u.shape[0] * u.shape[1] // TOK
    u_v = u.rearrange("b (n c p) d -> (b n) p c d", c=CH, p=P)
    out_v = out.rearrange("b (n c p) d -> (b n) p c d", c=CH, p=P)
    x1_d = nc.dram_tensor("x1_between_phases", (NS, P, CH, DM), F32).ap()
    mixer(nc, NS, u_v, win, wo, vec, x1_d)
    experts(nc, NS, x1_d, w1, w3, w2, out_v)


def kernel(**inputs):
    import numpy as np
    import concourse.bacc as bacc
    from concourse.bass_utils import run_bass_kernel_spmd

    x = {k: np.asarray(v) for k, v in inputs.items()}
    f32 = np.float32
    u = np.ascontiguousarray(x["L0_attn_u"])

    w = x["L0_attn_in_proj_w"].T
    w = np.concatenate([w[:, DI + XBC:], w[:, :DI], w[:, DI:DI + XBC]], axis=1)
    win = np.ascontiguousarray(w.reshape(KD, P, WIN).transpose(1, 0, 2))
    wo = np.ascontiguousarray(x["L0_attn_out_proj_w"].T.reshape(KI, P, DM).transpose(1, 0, 2))

    vec = np.zeros((P, V_ALL), f32)
    vec[:, V_TAP:V_BIAS] = x["L0_attn_conv_w"].reshape(NB, P, TAPS).transpose(1, 0, 2).reshape(P, -1)
    vec[:, V_BIAS:V_NORM] = x["L0_attn_conv_b"].reshape(NB, P).T
    vec[:, V_NORM:V_DT] = x["L0_attn_norm_w"].reshape(KI, P).T
    vec[:, V_DT:V_A] = x["L0_attn_dt_bias"]
    vec[:, V_A:V_D] = x["L0_attn_A_log"]
    vec[:, V_D:] = x["L0_attn_D"]

    def up(shared, routed, gate=None):
        cols = np.zeros((DM, FB, P), f32)
        cols[:, 0, :GROW] = shared[:, (SB - 1) * P:]
        cols[:, 1:SB] = shared[:, :(SB - 1) * P].reshape(DM, SB - 1, P)
        if gate is not None:
            cols[:, 0, GROW:GROW + E] = gate
        cols[:, SB:] = routed.transpose(1, 0, 2).reshape(DM, E, RB, FE // RB).transpose(0, 2, 1, 3)\
            .reshape(DM, RB, P)
        return np.ascontiguousarray(cols.reshape(KD, P, FB, P).transpose(1, 2, 0, 3).reshape(P, FB, KD * P))

    w1 = up(x["L0_ffn_sw1"], x["L0_ffn_rw1"], x["L0_ffn_gate_w"])
    w3 = up(x["L0_ffn_sw3"], x["L0_ffn_rw3"])
    w2 = np.zeros((P, FB, DM), f32)
    s2, r2 = x["L0_ffn_sw2"], x["L0_ffn_rw2"]
    w2[:GROW, 0] = s2[(SB - 1) * P:]
    w2[:, 1:SB] = s2[:(SB - 1) * P].reshape(SB - 1, P, DM).transpose(1, 0, 2)
    w2[:, SB:] = r2.reshape(E, RB, FE // RB, DM).transpose(0, 2, 1, 3).reshape(P, RB, DM)

    nc = bacc.Bacc("TRN2", target_bir_lowering=False, num_devices=1)
    arrays = dict(u_in=u, win_in=win, wo_in=wo, vec_in=vec, w1_in=w1, w3_in=w3, w2_in=w2)
    args = [nc.dram_tensor(name, a.shape, mybir.dt.from_np(a.dtype), kind="ExternalInput").ap()
            for name, a in arrays.items()]
    out = nc.dram_tensor("out", u.shape, F32, kind="ExternalOutput").ap()
    build(nc, *args, out)
    result = run_bass_kernel_spmd(nc, [arrays], core_ids=[0])
    return result.results[0]["out"]
```

```python
from contextlib import ExitStack

import concourse.bass as bass
from concourse import mybir

F32 = mybir.dt.float32
F32R = mybir.dt.float32r
ALU = mybir.AluOpType
ACT = mybir.ActivationFunctionType
AX = mybir.AxisListType

P = 128
DM = 256
KD = DM // P
DI = 512
H = 8
HD = DI // H
NST = 128
TAPS = 4
XBC = DI + 2 * NST
NB = XBC // P
IB, IC = 4, 5
ZH = (H + DI) // 2
ZD = 2 * ZH
WIN = ZD + XBC
KI = DI // P
TOK = 512
CH = TOK // P
SEQ = 2
EPS = 1e-5
E = 8
FE = 176
FS = 352
SB = -(-FS // P)
GROW = FS - (SB - 1) * P
RB = E * FE // P
FB = SB + RB
GROUPS = [(0, 1), (1, 3), (3, 7), (7, 11), (11, FB)]
V_TAP = 0
V_BIAS = V_TAP + NB * TAPS
V_NORM = V_BIAS + NB
V_DT = V_NORM + KI
V_A = V_DT + H
V_D = V_A + H
V_ALL = V_D + H


class Count:

    def __init__(self, handle, per, ahead):
        self.handle, self.per, self.ahead = handle, per, ahead


def need(eng, count, s, k):
    value = count.per * (s + 1 if count.ahead else s) + k
    if isinstance(value, int) and value <= 0:
        return
    eng.wait_ge(count.handle, value)


def need_alone(eng, count, s, k, carrier):
    need(eng, count, s, k)
    if not isinstance(s, int):
        eng.sem_inc(carrier.handle, 1)


def sig(ins, count):
    ins.then_inc(count.handle, 1)


def credit(eng, *counts):
    for c in counts:
        assert c.ahead
        eng.sem_inc(c.handle, c.per)


def product(nc, out, lh, ll, rh, rl, first, last):
    nc.tensor.matmul(out, ll, rh, start=first, stop=False)
    nc.tensor.matmul(out, lh, rl, start=False, stop=False)
    return nc.tensor.matmul(out, lh, rh, start=False, stop=last)


def flat(ap):
    return ap.rearrange("p a b -> p (a b)")


def mixer(nc, NS, u_v, win, wo, vec, x1_d, x1_first, x1_loaded, x1_stored):
    ctx = ExitStack()
    with ctx:
        def sb(name, shape, dt=F32):
            return ctx.enter_context(nc.sbuf_tensor(name, shape, dt))

        def sem(name, per=1, ahead=False):
            return Count(ctx.enter_context(nc.semaphore(name)), per, ahead)

        ident = sb("ident", [P, P])
        win_h = sb("win_h", [P, KD, WIN], F32R)
        win_l = sb("win_l", [P, KD, WIN], F32R)
        wo_n = sb("wo_n", [P, KI, DM])
        vecs = sb("vecs", [P, V_ALL])
        causal = sb("causal", [P, P])
        after_f = sb("after_f", [P, P])
        after = sb("after", [P, P], F32R)
        ones = sb("ones", [P, P])
        neg_half = sb("neg_half", [P, CH])
        exp_a = sb("exp_a", [P, H])
        u_ln = sb("u_ln", [P, CH, DM])
        bst = sb("bst", [P, CH, 6])
        mv = sb("mv", [P, CH, 2])
        ve = sb("ve", [P, CH])
        rstd = sb("rstd", [P, CH])
        xn = sb("xn", [P, CH, DM])
        xnt_h = sb("xnt_h", [P, KD, TOK], F32R)
        xnt_l = sb("xnt_l", [P, KD, TOK], F32R)
        sz = sb("sz", [P, 2, CH, DI])
        dt_raw = sb("dt_raw", [P, CH, H])
        raw = sb("raw", [P, 2, TAPS - 1 + TOK])
        halo = sb("halo", [P, NB, TAPS - 1])
        acc = sb("acc", [P, 2, TOK])
        xs = sb("xs", [P, 2, NB, TOK])
        v_dt = sb("v_dt", [P, CH, H])
        pos = sb("pos", [P, CH, H])
        nab = sb("nab", [P, CH, H])
        ex = sb("ex", [P, CH, H])
        den = sb("den", [P, CH, H])
        rcp = sb("rcp", [P, CH, H])
        ratio = sb("ratio", [P, CH, H])
        ratio2 = sb("ratio2", [P, CH, H])
        poly = sb("poly", [P, 2, CH, H])
        half_log = sb("half_log", [P, CH, H])
        dt = sb("dt", [P, 2, CH, H])
        a_f = sb("a_f", [P, CH, H])
        a_h = sb("a_h", [P, CH, H], F32R)
        a_l = sb("a_l", [P, CH, H], F32R)
        ecs = sb("ecs", [P, 2, 2, CH, H])
        v = sb("v", [P, CH, 2, H, P], F32R)
        decay = sb("decay", [P, CH, H, P])
        bt = sb("bt", [P, 2, NST])
        cbm = sb("cbm", [P, P])
        mix = sb("mix", [P, 2, H, P])
        xdt = sb("xdt", [P, 2, DI])
        xd = sb("xd", [P, 2, DI])
        xcd = sb("xcd", [P, DI])
        st = sb("st", [P, DI])
        st_dec = sb("st_dec", [P, DI])
        y = sb("y", [P, 2, DI])
        squares = sb("squares", [P, DI])
        ssq = sb("ssq", [P, CH])
        mse = sb("mse", [P, CH])
        rms = sb("rms", [P, CH])
        yt = sb("yt", [P, 2, KI, P])
        u_res = sb("u_res", [P, 2, CH, DM])
        mixed = sb("mixed", [P, CH, DM])
        x1 = sb("x1", [P, 2, CH, DM])
        stage = decay[:, :, :, :].rearrange("p a b c -> p (a b c)")
        win_f = stage[:, 0:KD * WIN].rearrange("p (k n) -> p k n", k=KD)
        wo_f = stage[:, KD * WIN:KD * WIN + KI * DM].rearrange("p (k n) -> p k n", k=KI)

        bank = [ctx.enter_context(nc.psum_tensor(f"bank{i}", [P, 512], F32)) for i in range(8)]

        vec_in = sem("vec_in")
        win_in = [sem(f"win_in{k}") for k in range(KD)]
        wo_in = sem("wo_in")
        const_step = sem("const_step")
        carrier = sem("carrier")
        consts = sem("consts")
        exp_a_ready = sem("exp_a_ready")
        wo_ready = sem("wo_ready")
        wh_ready = sem("wh_ready")
        wl_ready = sem("wl_ready")
        u_loaded = sem("u_loaded", 16)
        stats_ready = sem("stats_ready", CH)
        mv_ready = sem("mv_ready", CH)
        ve_ready = sem("ve_ready")
        rstd_ready = sem("rstd_ready")
        xn_ready = sem("xn_ready", CH)
        xnt_ps = sem("xnt_ps", KD)
        xnth_ready = sem("xnth_ready", KD)
        xntl_ready = sem("xntl_ready", KD)
        z_ps = sem("z_ps", 2 * CH)
        dt_copied = sem("dt_copied", CH)
        z_ready = sem("z_ready", 2 * CH)
        b_ps = sem("b_ps", NB)
        raw_ready = sem("raw_ready", NB)
        acc_ready = sem("acc_ready", NB)
        halo_in = sem("halo_in", NB)
        halo_out = sem("halo_out", NB, ahead=True)
        conv_step = sem("conv_step", 3 * NB, ahead=True)
        xs_ready = sem("xs_ready", NB)
        DT_NAB, DT_A, DT_ALL = 3, 16, 18
        dt_step = sem("dt_step", DT_ALL)
        ex_ready = sem("ex_ready")
        cs_ps = sem("cs_ps")
        ecs_ready = sem("ecs_ready")
        v_ready = sem("v_ready", 2 * CH)
        seg_ps = sem("seg_ps", 2 * CH)
        decay_ready = sem("decay_ready", 2 * CH)
        cb_ps = sem("cb_ps", CH)
        bt_ready = sem("bt_ready", CH, ahead=True)
        cbm_ready = sem("cbm_ready", CH, ahead=True)
        x_ps = sem("x_ps", CH)
        xdt_ready = sem("xdt_ready", CH)
        xd_ready = sem("xd_ready", CH, ahead=True)
        mix_ready = sem("mix_ready", CH)
        xcd_ready = sem("xcd_ready", CH)
        yo_ps = sem("yo_ps", CH)
        yd_ps = sem("yd_ps", CH)
        sp_ps = sem("sp_ps", CH)
        st_decayed = sem("st_decayed", CH)
        st_ready = sem("st_ready", CH, ahead=True)
        y_off = sem("y_off", CH)
        y_sum = sem("y_sum", CH, ahead=True)
        y_skip = sem("y_skip", CH, ahead=True)
        y_gated = sem("y_gated", CH)
        ssq_ready = sem("ssq_ready", CH, ahead=True)
        mse_ready = sem("mse_ready", CH)
        rms_ready = sem("rms_ready", CH)
        yt_ps = sem("yt_ps", CH)
        yt_ready = sem("yt_ready", CH)
        op_ps = sem("op_ps", CH)
        mixed_ready = sem("mixed_ready", CH, ahead=True)
        x1_ready = sem("x1_ready", CH, ahead=True)
        res_loaded = [sem("res_loaded0"), sem("res_loaded1")]

        ORDER = {
            "PE": "A0 X0 Y0 A1 Z0 Y1 A2 Z1 Z2 Z3 B0 T0 B1 Y2 A3 O0 T1 B2 B3 O1 B4 B5 Y3 T2 S0 O2 "
                  "S1 S2 T3 E0 S3 O3",
            "ACT": "A0 X0 A1 Z0 A2 Z1 Z2 Z3 D0 B0 T0 B1 A3 O0 T1 B2 B3 B4 B5 O1 T2 C0 S0 O2 S1 S2 "
                   "T3 E0 S3 O3",
            "DVE": "L0 A0 X0 Y0 A1 N0 Y1 T0 A2 T1 D0 B0 Y2 B1 T2 A3 B2 B3 B4 B5 Y3 T3",
            "POOL": "A0 Y0 L0 Y1 A1 W0 W1 A2 Y2 B0 T0 B1 V0 V1 W2 T1 B2 V2 Y3 B3 V3 A3 B4 V4 O0 B5 "
                    "V5 T2 V6 W3 V7 O1 O2 T3 O3",
        }
        FRONT = "X0 L0 Z0 Z1 N0 Z2 Z3 D0 B0 V0 B1 V1 B2 V2 B3 V3 B4 V4 V5 B5 S0 E0 S1 C0 V6 V7 S2 S3"

        def step(piece, order, i, par, left):
            for name in order.split():
                if left >= (1 if name[0] in "XZDBCEVS" else 2 if name[0] in "LN" else 0):
                    piece(name[0], int(name[1]), i, par, left)

        def run(eng, name, piece):
            step(piece, FRONT, -1, 1, 2)
            with eng.Fori(0, NS // 2 - 1) as i:
                for par in range(2):
                    step(piece, ORDER[name], i, par, 2)
            for par in range(2):
                step(piece, ORDER[name], NS // 2 - 1, par, 1 - par)

        block = ctx.enter_context(nc.Block())

        @block.sync
        def _(sp):
            def load_ln(n):
                need(sp, xn_ready, n - 1, CH)
                sp.dma_start(u_ln[:, :, :], u_v[n]).then_inc(u_loaded.handle, 16)

            def load_res(i, par):
                need(sp, x1_ready, 2 * i + par - 2, CH)
                sp.dma_start(u_res[:, par], u_v[2 * i + par]).then_inc(res_loaded[par].handle, 16)

            def store_x1(i, par):
                need(sp, x1_ready, 2 * i + par, CH)
                sp.dma_start(x1_d[2 * i + par], x1[:, par]).then_inc(x1_stored[par].handle, 16)

            load_ln(0)
            sp.dma_start(vecs[:, :], vec).then_inc(vec_in.handle, 16)
            for k in range(KD):
                sp.dma_start(win_f[:, k, :], win[:, k, :]).then_inc(win_in[k].handle, 16)
            sp.dma_start(wo_f, wo).then_inc(wo_in.handle, 16)
            load_ln(1)
            load_res(0, 0)
            load_res(0, 1)
            load_ln(2)
            with sp.Fori(0, NS // 2 - 2) as i:
                for par in range(2):
                    load_ln(2 * i + par + 3)
                    store_x1(i, par)
                    load_res(i + 1, par)
            load_ln(NS - 1)
            for par in range(2):
                store_x1(NS // 2 - 2, par)
                load_res(NS // 2 - 1, par)
            sp.wait_ge(x1_stored[0].handle, 32)
            sp.dma_start(x1_first, x1_d[0]).then_inc(x1_loaded[0].handle, 16)
            for par in range(2):
                store_x1(NS // 2 - 1, par)

        @block.tensor
        def _(pe):
            def piece(kind, j, i, par, left):
                s = 2 * i + par
                n = s + 1
                tok = slice(j * P, (j + 1) * P)
                before = (s, j) if j else (s - 1, CH)
                if kind == "X":
                    for k in range(KD):
                        if k == 0:
                            need(pe, cbm_ready, s, 1)
                            need(pe, bt_ready, s, 1)
                        else:
                            need(pe, xd_ready, s, 1)
                        for c in range(CH):
                            if k == 0:
                                need(pe, xn_ready, n, c + 1)
                            last = nc.tensor.transpose(bank[2 + k][:, c * P:(c + 1) * P],
                                                       xn[:, c, k * P:(k + 1) * P], ident[:, :])
                        sig(last, xnt_ps)
                    if isinstance(n, int) and n == 0:
                        pe.wait_ge(wh_ready.handle, KD)
                        pe.wait_ge(wl_ready.handle, KD)
                elif kind == "E":
                    need(pe, y_off, s, CH)
                    need(pe, dt_step, n, DT_A)
                    for k, mask in enumerate((ones, causal)):
                        last = nc.tensor.matmul(bank[4][:, k * CH * H:(k + 1) * CH * H], mask[:, :],
                                                flat(a_f[:, :, :]), start=True, stop=True)
                    sig(last, cs_ps)
                elif kind == "S":
                    need(pe, v_ready, n, 2 * j + 2)
                    for g in range(2):
                        if j == 0:
                            need(pe, acc_ready, n, NB - 1 + g)
                        else:
                            need(pe, decay_ready, n, 2 * (j - 1) + g + 1)
                        hs = slice(g * H // 2, (g + 1) * H // 2)
                        nc.tensor.matmul(bank[g][:, :], after[:, :], flat(v[:, j, 0, hs]),
                                         start=True, stop=False)
                        sig(nc.tensor.matmul(bank[g][:, :], after[:, :], flat(v[:, j, 1, hs]),
                                             start=False, stop=True), seg_ps)
                elif kind == "Z":
                    if j == 0:
                        need(pe, xnth_ready, n, KD)
                        need(pe, xntl_ready, n, KD)
                    for g in range(2):
                        if j == 0:
                            need(pe, decay_ready, s, 2 * CH - 1 + g)
                        else:
                            need(pe, z_ready, n, 2 * (j - 1) + g + 1)
                        cols = slice(g * ZH, (g + 1) * ZH)
                        for k in range(KD):
                            last = product(nc, bank[g][:, 0:ZH], xnt_h[:, k, tok], xnt_l[:, k, tok],
                                           win_h[:, k, cols], win_l[:, k, cols], k == 0, k == KD - 1)
                        sig(last, z_ps)
                elif kind == "B":
                    g = j % 2
                    if j < 2:
                        need(pe, z_ready, n, 2 * (CH - 1) + g + 1)
                    else:
                        need(pe, acc_ready, n, j - 1)
                    cols = slice(ZD + j * P, ZD + (j + 1) * P)
                    for k in range(KD):
                        last = product(nc, bank[g][:, :], win_h[:, k, cols], win_l[:, k, cols],
                                       xnt_h[:, k, :], xnt_l[:, k, :], k == 0, k == KD - 1)
                    sig(last, b_ps)
                elif kind == "A":
                    if j == 0:
                        need(pe, xs_ready, s, NB)
                    normalised_between = j == 1 and left >= 1
                    if normalised_between:
                        need(pe, xntl_ready, n, KD)
                    else:
                        need(pe, cbm_ready, *before)
                        need(pe, bt_ready, *before)
                    nc.tensor.matmul(bank[2][:, 0:P], xs[:, par, IB, tok], xs[:, par, IC, tok],
                                     start=True, stop=True)
                    sig(nc.tensor.transpose(bank[2][:, P:2 * P], xs[:, par, IB, tok], ident[:, :]),
                        cb_ps)
                    if not normalised_between:
                        need(pe, xd_ready, *before)
                    for b in range(KI):
                        last = nc.tensor.transpose(bank[3][:, b * P:(b + 1) * P],
                                                   xs[:, par, b, tok], ident[:, :])
                    sig(last, x_ps)
                elif kind == "Y":
                    if j == 0:
                        need(pe, ecs_ready, s, 1)
                    else:
                        need(pe, y_off, s, j)
                    need(pe, st_ready, *before)
                    sig(nc.tensor.matmul(bank[4][:, :], xs[:, par, IC, tok], st[:, :],
                                         start=True, stop=True), yo_ps)
                    need(pe, bt_ready, s, j + 1)
                    need(pe, xcd_ready, s, j + 1)
                    sig(nc.tensor.matmul(bank[6][:, :], bt[:, j % 2, :], xcd[:, :],
                                         start=True, stop=True), sp_ps)
                    need(pe, mix_ready, s, j + 1)
                    need(pe, xdt_ready, s, j + 1)
                    need(pe, y_sum, *before)
                    for h in range(H):
                        cols = slice(h * HD, min((h + 2) * HD, DI))
                        last = nc.tensor.matmul(bank[5][:, cols], mix[:, j % 2, h, :],
                                                xdt[:, j % 2, cols], start=True, stop=True)
                    sig(last, yd_ps)
                elif kind == "T":
                    need(pe, y_gated, s, j + 1)
                    need(pe, mixed_ready, *before)
                    for b in range(KI):
                        last = nc.tensor.transpose(bank[7][:, b * P:(b + 1) * P],
                                                   y[:, j % 2, b * P:(b + 1) * P], ident[:, :])
                    sig(last, yt_ps)
                elif kind == "O":
                    if j == 0:
                        pe.wait_ge(wo_ready.handle, KI)
                    need(pe, yt_ready, s, j + 1)
                    for b in range(KI):
                        last = nc.tensor.matmul(bank[7][:, 0:DM], yt[:, j % 2, b, :], wo_n[:, b, :],
                                                start=b == 0, stop=b == KI - 1)
                    sig(last, op_ps)

            pe.wait_ge(consts.handle, 3)
            run(pe, "PE", piece)

        @block.scalar
        def _(act):
            A = nc.scalar.activation

            def silu(n, npar, b):
                need(act, conv_step, n, 3 * (b + 1))
                sig(A(xs[:, npar, b, :], acc[:, b % 2, :], ACT.Silu), xs_ready)

            def piece(kind, j, i, par, left):
                s = 2 * i + par
                n, npar = s + 1, 1 - par
                if kind == "X":
                    for k in range(KD):
                        need(act, xnt_ps, n, k + 1)
                        sig(A(xnt_h[:, k, :], bank[2 + k][:, :], ACT.Copy), xnth_ready)
                elif kind == "D":
                    need(act, dt_step, n, DT_NAB)
                    sig(A(ex[:, :, :], nab[:, :, :], ACT.Exp), ex_ready)
                elif kind == "E":
                    need(act, cs_ps, n, 1)
                    sig(A(ecs[:, npar].rearrange("p a c h -> p (a c h)"), bank[4][:, 0:2 * CH * H],
                          ACT.Exp), ecs_ready)
                elif kind == "S":
                    for g in range(2):
                        need(act, seg_ps, n, 2 * j + g + 1)
                        sig(A(flat(decay[:, j, g * H // 2:(g + 1) * H // 2]), bank[g][:, :], ACT.Exp),
                            decay_ready)
                elif kind == "Z":
                    need(act, z_ps, n, 2 * j + 1)
                    sig(A(dt_raw[:, j, :], bank[0][:, 0:H], ACT.Copy), dt_copied)
                    sig(A(sz[:, npar, j, 0:ZH - H], bank[0][:, H:ZH], ACT.Silu), z_ready)
                    need(act, z_ps, n, 2 * j + 2)
                    sig(A(sz[:, npar, j, ZH - H:DI], bank[1][:, 0:ZH], ACT.Silu), z_ready)
                elif kind == "B":
                    g = j % 2
                    if j >= 2:
                        need(act, conv_step, n, 3 * (j - 1))
                        need(act, halo_out, n, j - 1)
                        need(act, xs_ready, n, j - 1)
                    else:
                        need(act, conv_step, n - 1, 3 * (NB - 1 + j))
                        need(act, halo_out, n - 1, NB - 1 + j)
                        need(act, xs_ready, n - 1, NB - 1 + j)
                    need(act, b_ps, n, j + 1)
                    sig(A(raw[:, g, TAPS - 1:], bank[g][:, :], ACT.Copy), raw_ready)
                    tap = V_TAP + j * TAPS + TAPS - 1
                    sig(A(acc[:, g, :], bank[g][:, :], ACT.Identity, bias=vecs[:, V_BIAS + j:V_BIAS + j + 1],
                          scale=vecs[:, tap:tap + 1]), acc_ready)
                    if j:
                        silu(n, npar, j - 1)
                elif kind == "C":
                    silu(n, npar, NB - 1)
                elif kind == "A":
                    need(act, cb_ps, s, j + 1)
                    sig(A(bt[:, j % 2, :], bank[2][:, P:2 * P], ACT.Copy), bt_ready)
                elif kind == "T":
                    need(act, y_gated, s, j + 1)
                    sig(A(squares[:, :], y[:, j % 2, :], ACT.Square, accum_out=ssq[:, j:j + 1]),
                        ssq_ready)
                    need(act, yt_ps, s, j + 1)
                    sig(A(flat(yt[:, j % 2]), bank[7][:, :], ACT.Copy), yt_ready)
                elif kind == "O":
                    need(act, x1_ready, s - 1, j + 1)
                    need(act, rms_ready, s, j + 1)
                    need(act, op_ps, s, j + 1)
                    sig(A(mixed[:, j, :], bank[7][:, 0:DM], ACT.Identity, scale=rms[:, j:j + 1]),
                        mixed_ready)

            credit(act, bt_ready, mixed_ready, ssq_ready)
            for k in range(KD):
                act.wait_ge(win_in[k].handle, 16)
                A(win_h[:, k, :], win_f[:, k, :], ACT.Copy).then_inc(wh_ready.handle, 1)
            act.wait_ge(vec_in.handle, 16)
            A(exp_a[:, :], vecs[:, V_A:V_A + H], ACT.Exp).then_inc(exp_a_ready.handle, 1)
            run(act, "ACT", piece)

        @block.vector
        def _(dve):
            V = nc.vector

            def statistics(n):
                need(dve, u_loaded, n, 16)
                for c in range(CH):
                    sig(V.bn_stats(bst[:, c, :], u_ln[:, c, :]), stats_ready)
                for c in range(CH):
                    need_alone(dve, stats_ready, n, c + 1, carrier)
                    sig(V.bn_aggr(mv[:, c, :], bst[:, c, :]), mv_ready)

            def normalise(n):
                need(dve, rstd_ready, n, 1)
                need(dve, xnt_ps, n - 1, KD)
                for c in range(CH):
                    sig(V.tensor_scalar(xn[:, c, :], u_ln[:, c, :], mv[:, c, 0:1], rstd[:, c:c + 1],
                                        ALU.subtract, ALU.mult), xn_ready)

            def step_sizes(n, npar):
                done = [0]

                def link(ins):
                    sig(ins, dt_step)
                    done[0] += 1
                    need(dve, dt_step, n, done[0])

                over_chunks = lambda ap: ap.unsqueeze(1).to_broadcast([P, CH, H])
                need(dve, dt_copied, n, CH)
                link(V.tensor_tensor(v_dt[:, :, :], dt_raw[:, :, :], over_chunks(vecs[:, V_DT:V_DT + H]),
                                     ALU.add))
                link(V.tensor_scalar(pos[:, :, :], v_dt[:, :, :], 0.0, None, ALU.max))
                link(V.scalar_tensor_tensor(nab[:, :, :], v_dt[:, :, :], -1.0, v_dt[:, :, :],
                                            ALU.mult, ALU.min))
                assert done[0] == DT_NAB
                need(dve, ex_ready, n, 1)
                link(V.tensor_scalar(den[:, :, :], ex[:, :, :], 2.0, None, ALU.add))
                link(V.reciprocal(rcp[:, :, :], den[:, :, :]))
                link(V.tensor_tensor(ratio[:, :, :], ex[:, :, :], rcp[:, :, :], ALU.mult))
                link(V.tensor_tensor(ratio2[:, :, :], ratio[:, :, :], ratio[:, :, :], ALU.mult))
                link(V.tensor_scalar(poly[:, 1], ratio2[:, :, :], 1.0 / 13, None, ALU.mult))
                for k, odd in ((1, 11), (0, 9), (1, 7), (0, 5), (1, 3)):
                    link(V.scalar_tensor_tensor(poly[:, (k + 1) % 2], poly[:, k % 2], 1.0 / odd,
                                                ratio2[:, :, :], ALU.add, ALU.mult))
                link(V.scalar_tensor_tensor(half_log[:, :, :], poly[:, 0], 1.0, ratio[:, :, :],
                                            ALU.add, ALU.mult))
                link(V.scalar_tensor_tensor(dt[:, npar], half_log[:, :, :], 2.0, pos[:, :, :],
                                            ALU.mult, ALU.add))
                need(dve, cs_ps, n - 1, 1)
                need(dve, v_ready, n - 1, 2 * CH)
                link(V.scalar_tensor_tensor(a_f[:, :, :], dt[:, npar], -1.0, over_chunks(exp_a[:, :]),
                                            ALU.mult, ALU.mult))
                assert done[0] == DT_A
                link(V.tensor_copy(a_h[:, :, :], a_f[:, :, :]))
                link(V.tensor_tensor(a_l[:, :, :], a_f[:, :, :], a_h[:, :, :].bitcast(F32), ALU.subtract))
                assert done[0] == DT_ALL

            def heads(ap):
                return ap.rearrange("p (h d) -> p h d", h=H)

            def per_head(ap):
                return ap.unsqueeze(2).to_broadcast([P, H, HD])

            def piece(kind, j, i, par, left):
                s = 2 * i + par
                n = s + 1
                two_before = (s, j - 1) if j >= 2 else (s - 1, CH - 1 + j)
                if kind == "X":
                    for k in range(KD):
                        need(dve, xnth_ready, n, k + 1)
                        sig(V.tensor_tensor(xnt_l[:, k, :], bank[2 + k][:, :],
                                            xnt_h[:, k, :].bitcast(F32), ALU.subtract), xntl_ready)
                elif kind == "L":
                    statistics(s + 2)
                elif kind == "N":
                    normalise(s + 2)
                elif kind == "D":
                    step_sizes(n, 1 - par)
                elif kind == "B":
                    g = j % 2
                    need(dve, raw_ready, n, j + 1)
                    need(dve, halo_in, n, j + 1)
                    need(dve, acc_ready, n, j + 1)
                    for t in range(TAPS - 1):
                        if t:
                            need(dve, conv_step, n, 3 * j + t)
                        tap = V_TAP + j * TAPS + t
                        sig(V.scalar_tensor_tensor(acc[:, g, :], raw[:, g, t:t + TOK],
                                                   vecs[:, tap:tap + 1], acc[:, g, :],
                                                   ALU.mult, ALU.add), conv_step)
                elif kind == "A":
                    need(dve, bt_ready, s, j + 1)
                    sig(V.tensor_tensor(cbm[:, :], bank[2][:, 0:P], causal[:, :], ALU.mult), cbm_ready)
                    need(dve, x_ps, s, j + 1)
                    sig(V.tensor_tensor(heads(xdt[:, j % 2, :]), heads(bank[3][:, :]),
                                        per_head(dt[:, par, j, :]), ALU.mult), xdt_ready)
                    need(dve, y_skip, *two_before)
                    sig(V.tensor_tensor(heads(xd[:, j % 2, :]), heads(bank[3][:, :]),
                                        per_head(vecs[:, V_D:V_D + H]), ALU.mult), xd_ready)
                    need(dve, cbm_ready, s, j + 1)
                    need(dve, decay_ready, s, 2 * j + 2)
                    sig(V.tensor_tensor(mix[:, j % 2], decay[:, j],
                                        cbm[:, :].unsqueeze(1).to_broadcast([P, H, P]), ALU.mult),
                        mix_ready)
                elif kind == "Y":
                    need(dve, ecs_ready, s, 1)
                    need(dve, ssq_ready, *two_before)
                    need(dve, yo_ps, s, j + 1)
                    sig(V.tensor_tensor(heads(y[:, j % 2, :]), heads(bank[4][:, :]),
                                        per_head(ecs[:, par, 1, j, :]), ALU.mult), y_off)
                    need(dve, st_decayed, s, j + 1)
                    need(dve, sp_ps, s, j + 1)
                    if par == SEQ - 1 and j == CH - 1:
                        sig(V.memset(st[:, :], 0.0), st_ready)
                    else:
                        sig(V.tensor_tensor(st[:, :], st_dec[:, :], bank[6][:, :], ALU.add), st_ready)
                    need(dve, y_off, s, j + 1)
                    need(dve, yd_ps, s, j + 1)
                    sig(V.tensor_tensor(y[:, j % 2, :], y[:, j % 2, :], bank[5][:, :], ALU.add), y_sum)
                elif kind == "T":
                    need(dve, y_skip, s, j + 1)
                    sig(V.tensor_tensor(y[:, j % 2, :], y[:, j % 2, :], sz[:, par, j, :], ALU.mult),
                        y_gated)

            credit(dve, conv_step, cbm_ready, xd_ready, st_ready, y_sum)
            V.memset(st[:, :], 0.0).then_inc(consts.handle, 1)
            statistics(0)
            normalise(0)
            for k in range(KD):
                dve.wait_ge(wh_ready.handle, k + 1)
                V.tensor_tensor(win_l[:, k, :], win_f[:, k, :], win_h[:, k, :].bitcast(F32),
                                ALU.subtract).then_inc(wl_ready.handle, 1)
            dve.wait_ge(vec_in.handle, 16)
            dve.wait_ge(wo_in.handle, 16)
            for b in range(KI):
                V.tensor_scalar(wo_n[:, b, :], wo_f[:, b, :], vecs[:, V_NORM + b:V_NORM + b + 1], None,
                                ALU.mult).then_inc(wo_ready.handle, 1)
            dve.wait_ge(exp_a_ready.handle, 1)
            dve.wait_ge(consts.handle, 3)
            run(dve, "DVE", piece)

        @block.gpsimd
        def _(pool):
            G = nc.gpsimd

            def rstd_of(n):
                need_alone(pool, mv_ready, n, CH, carrier)
                sig(G.tensor_scalar(ve[:, :], mv[:, :, 1], EPS, None, ALU.add), ve_ready)
                need(pool, ve_ready, n, 1)
                sig(G.tensor_tensor(rstd[:, :], ve[:, :], neg_half[:, :], ALU.pow), rstd_ready)

            def piece(kind, j, i, par, left):
                s = 2 * i + par
                n, npar = s + 1, 1 - par
                if kind == "V":
                    need(pool, dt_step, n, DT_ALL)
                    c, src = j // 2, (a_h, a_l)[j % 2]
                    need(pool, seg_ps, n - 1, 2 * c + 2)
                    sig(G.tensor_tensor(v[:, c, j % 2], causal[:, :].unsqueeze(1).to_broadcast([P, H, P]),
                                        src[:, c, :].bitcast(F32).unsqueeze(2).to_broadcast([P, H, P]),
                                        ALU.mult), v_ready)
                elif kind == "L":
                    rstd_of(s + 2)
                elif kind == "B":
                    g = j % 2
                    need_alone(pool, conv_step,
                               *((n, 3 * (j - 1)) if j >= 2 else (n - 1, 3 * (NB - 1 + j))), carrier)
                    if npar == 0:
                        sig(G.memset(raw[:, g, 0:TAPS - 1], 0.0), halo_in)
                    else:
                        need_alone(pool, halo_out, n - 1, j + 1, carrier)
                        sig(G.tensor_copy(raw[:, g, 0:TAPS - 1], halo[:, j, :]), halo_in)
                    need(pool, halo_in, n, j + 1)
                    need_alone(pool, raw_ready, n, j + 1, carrier)
                    sig(G.tensor_copy(halo[:, j, :], raw[:, g, TOK:TOK + TAPS - 1]), halo_out)
                elif kind == "A":
                    need(pool, xdt_ready, s, j + 1)
                    need(pool, decay_ready, s, 2 * j + 2)
                    sig(G.tensor_tensor(xcd[:, :].rearrange("p (h d) -> p h d", h=H),
                                        xdt[:, j % 2, :].rearrange("p (h d) -> p h d", h=H),
                                        decay[:, j, :, P - 1:P].to_broadcast([P, H, HD]), ALU.mult),
                        xcd_ready)
                elif kind == "Y":
                    need(pool, ecs_ready, s, 1)
                    need(pool, st_ready, *((s, j) if j else (s - 1, CH)))
                    sig(G.tensor_tensor(st_dec[:, :].rearrange("p (h d) -> p h d", h=H),
                                        st[:, :].rearrange("p (h d) -> p h d", h=H),
                                        ecs[:, par, 0, j, :].unsqueeze(2).to_broadcast([P, H, HD]),
                                        ALU.mult), st_decayed)
                elif kind == "W":
                    need(pool, y_sum, s, j + 1)
                    sig(G.tensor_tensor(y[:, j % 2, :], y[:, j % 2, :], xd[:, j % 2, :], ALU.add), y_skip)
                elif kind == "T":
                    need_alone(pool, ssq_ready, s, j + 1, carrier)
                    sig(G.tensor_scalar(mse[:, j:j + 1], ssq[:, j:j + 1], 1.0 / DI, EPS,
                                        ALU.mult, ALU.add), mse_ready)
                    need(pool, mse_ready, s, j + 1)
                    sig(G.tensor_tensor(rms[:, j:j + 1], mse[:, j:j + 1], neg_half[:, 0:1], ALU.pow),
                        rms_ready)
                elif kind == "O":
                    if j == 0:
                        pool.wait_ge(res_loaded[par].handle, 16 * (i + 1))
                        pool.wait_ge(x1_stored[par].handle, 16 * (i + 1))
                    need(pool, mixed_ready, s, j + 1)
                    sig(G.tensor_tensor(x1[:, par, j, :], mixed[:, j, :], u_res[:, par, j, :],
                                        ALU.add), x1_ready)

            credit(pool, halo_out, x1_ready, y_skip)
            for par in range(2):
                pool.sem_inc(x1_stored[par].handle, 16)
            for m, value in ((ident, 0.0), (causal, 1.0), (after_f, 1.0), (ones, 1.0), (neg_half, -0.5)):
                G.memset(m[:, :], value).then_inc(const_step.handle, 1)
            pool.wait_ge(const_step.handle, 5)
            for m, op, fill, a, b in ((ident, ALU.not_equal, 1.0, -1, 1), (causal, ALU.is_ge, 0.0, 1, -1),
                                      (after_f, ALU.is_gt, 0.0, -1, 1)):
                G.affine_select(out=m[:, :], in_=m[:, :], compare_op=op, fill=fill, base=0,
                                pattern=[[a, P]], channel_multiplier=b).then_inc(const_step.handle, 1)
            pool.wait_ge(const_step.handle, 8)
            G.tensor_copy(after[:, :], after_f[:, :]).then_inc(const_step.handle, 1)
            pool.wait_ge(const_step.handle, 9)
            G.memset(halo[:, :, :], 0.0).then_inc(consts.handle, 2)
            rstd_of(0)
            run(pool, "POOL", piece)


def experts(nc, NS, x1_d, x1_first, x1_loaded, x1_stored, w1, w3, w2, out_v):
    ctx = ExitStack()
    with ctx:
        def sb(name, shape, dt=F32):
            return ctx.enter_context(nc.sbuf_tensor(name, shape, dt))

        def sem(name, per=1, ahead=False):
            return Count(ctx.enter_context(nc.semaphore(name)), per, ahead)

        w1_f = sb("w1_f", [P, FB, KD * P])
        w3_f = sb("w3_f", [P, FB, KD * P])
        w2_f = sb("w2_f", [P, FB, DM])
        w1_h = sb("w1_h", [P, FB, KD * P], F32R)
        w1_l = sb("w1_l", [P, FB, KD * P], F32R)
        w3_h = sb("w3_h", [P, FB, KD * P], F32R)
        w3_l = sb("w3_l", [P, FB, KD * P], F32R)
        w2_h = sb("w2_h", [P, FB, DM], F32R)
        w2_l = sb("w2_l", [P, FB, DM], F32R)
        ident = sb("ident2", [P, P])
        sel_f = sb("sel_f", [2 * E, 2, P])
        sel = sb("sel", [2 * E, P], F32R)
        neg_half = sb("neg_half2", [P, CH])
        rank = sb("rank", [P, E])
        x1 = [x1_first, sb("x1_in1", [P, CH, DM])[:, :, :]]
        bst = sb("bst2", [P, CH, 6])
        mv = sb("mv2", [P, CH, 2])
        ve = sb("ve2", [P, CH])
        rstd = sb("rstd2", [P, CH])
        xn = sb("xn2", [P, CH, DM])
        xt_h = sb("xt_h", [P, 2, KD, TOK], F32R)
        xt_l = sb("xt_l", [P, 2, KD, TOK], F32R)
        lg = sb("lg", [P, TOK])
        lgt = sb("lgt", [P, CH, E])
        shifted = sb("shifted", [P, CH, E])
        ep = sb("ep", [P, CH, E])
        score = sb("score", [P, CH, E])
        top = sb("top", [P, CH])
        total = sb("total", [P, CH])
        inv = sb("inv", [P, CH])
        tied = sb("tied", [P, CH, E])
        tied_rank = sb("tied_rank", [P, CH, E])
        best_rank = sb("best_rank", [P, CH])
        pick1 = sb("pick1", [P, CH, E])
        pick2 = sb("pick2", [P, CH, E])
        rest = sb("rest", [P, CH, E])
        cw = sb("cw", [P, CH, E])
        cw_r = sb("cw_r", [P, CH, E], F32R)
        cw_parts = sb("cw_parts", [P, CH, 2 * E])
        cwt = sb("cwt", [2 * E, TOK], F32R)
        cwb = sb("cwb", [P, TOK])
        act1 = sb("act1", [P, 2, TOK])
        g = sb("g", [P, 2, TOK])
        g_h = sb("g_h", [P, 2, TOK], F32R)
        g_l = sb("g_l", [P, 2, TOK], F32R)
        ob = sb("ob", [P, CH, DM])
        bank = [ctx.enter_context(nc.psum_tensor(f"ebank{k}", [P, 512], F32)) for k in range(8)]

        w_in = [sem(f"w_in{k}") for k in range(len(GROUPS))]
        group_of = [k for k, (a, b) in enumerate(GROUPS) for _ in range(a, b)]
        wh_ready = sem("e_wh_ready")
        wl_ready = sem("e_wl_ready")
        const_step = sem("e_const_step")
        carrier = sem("e_carrier")
        consts = sem("e_consts")
        stats_ready = sem("e_stats_ready", CH)
        mv_ready = sem("e_mv_ready", CH)
        ve_ready = sem("e_ve_ready")
        rstd_ready = sem("e_rstd_ready")
        xn_ready = sem("e_xn_ready", CH)
        xt_ps = sem("xt_ps", KD)
        xth_ready = sem("xth_ready", KD)
        xtl_ready = sem("xtl_ready", KD)
        h1_ps = sem("h1_ps", FB)
        h3_ps = sem("h3_ps", FB)
        act_ready = sem("act_ready", FB)
        lg_ready = sem("lg_ready")
        lg_ps = sem("lg_ps")
        lgt_ready = sem("lgt_ready")
        R_SHIFT, R_PART, R_ALL = 2, 5, 21
        route = sem("route", R_ALL)
        ep_ready = sem("ep_ready")
        cwt_ps = sem("cwt_ps")
        cwt_ready = sem("cwt_ready")
        cwb_ps = sem("cwb_ps")
        cwb_ready = sem("cwb_ready")
        prod_ready = sem("prod_ready", FB)
        g_ready = sem("g_ready", RB)
        gh_ready = sem("gh_ready", FB)
        gl_ready = sem("gl_ready", FB)
        down_ps = sem("down_ps", FB)
        ob_ready = sem("ob_ready", 2)
        stored = sem("stored", 16, ahead=True)

        ORDER = ["F0", "H0", f"D{FB - 1}", "K0", "G0", "F1", "R0", "H1", "D0", "F2", "H2", "D1",
                 "C0", "F3", "S0", "H3", "D2"]
        for j in range(4, FB):
            ORDER += [f"F{j}", f"H{j}"] + {5: ["L0"], 7: ["N0"], 9: ["X0"]}.get(j, []) + [f"D{j - 1}"]

        def step(piece, n, par, loads, first, last):
            for name in ORDER:
                kind, j = name[0], int(name[1:])
                before = kind == "K" or name == f"D{FB - 1}"
                if (before and first) or (kind in "LNX" and last):
                    continue
                piece(kind, j, n - 1 if before else n, 1 - par if before else par,
                      loads if kind == "L" else None, first)

        def run(eng, piece):
            step(piece, 0, 0, 1, True, False)
            with eng.Fori(0, NS // 2 - 1) as i:
                step(piece, 2 * i + 1, 1, i + 2, False, False)
                step(piece, 2 * i + 2, 0, i + 2, False, False)
            step(piece, NS - 1, 1, None, False, True)
            for kind, j in (("D", FB - 1), ("K", 0)):
                piece(kind, j, NS - 1, 1, None, False)

        block = ctx.enter_context(nc.Block())

        @block.sync
        def _(sp):
            def load(n, par):
                need(sp, ob_ready, n - 2, 2)
                sp.dma_start(x1[par], x1_d[n]).then_inc(x1_loaded[par].handle, 16)

            def store(n):
                need(sp, ob_ready, n, 2)
                sp.dma_start(out_v[n], ob[:, :, :]).then_inc(stored.handle, 16)

            credit(sp, stored)
            for k, (a, b) in enumerate(GROUPS):
                for dst, src in ((w1_f, w1), (w3_f, w3), (w2_f, w2)):
                    sp.dma_start(dst[:, a:b, :], src[:, a:b, :]).then_inc(w_in[k].handle, 16)
            for par in range(2):
                sp.wait_ge(x1_stored[par].handle, 16 * (NS // 2 + 1))
            load(1, 1)
            with sp.Fori(0, NS // 2 - 1) as i:
                for par in range(2):
                    store(2 * i + par)
                    load(2 * i + par + 2, par)
            store(NS - 2)
            store(NS - 1)
            need(sp, stored, NS - 1, 16)

        @block.tensor
        def _(pe):
            def transposes(n, par):
                for k in range(KD):
                    for c in range(CH):
                        if k == 0:
                            need(pe, xn_ready, n, c + 1)
                        last = nc.tensor.transpose(bank[6 + k][:, c * P:(c + 1) * P],
                                                   xn[:, c, k * P:(k + 1) * P], ident[:, :])
                    sig(last, xt_ps)

            def piece(kind, j, n, par, loads, first):
                if kind == "F":
                    b = j % 2
                    if j == 0:
                        need(pe, xth_ready, n, KD)
                        need(pe, xtl_ready, n, KD)
                    if first:
                        pe.wait_ge(wh_ready.handle, 3 * (j + 1))
                        pe.wait_ge(wl_ready.handle, 3 * (j + 1))
                    need(pe, act_ready, *((n, j - 1) if j >= 2 else (n - 1, FB - 1 + j)))
                    if j == 2:
                        need(pe, lg_ready, n, 1)
                    for k in range(KD):
                        cols = slice(k * P, (k + 1) * P)
                        last = product(nc, bank[2 + b][:, :], w1_h[:, j, cols], w1_l[:, j, cols],
                                       xt_h[:, par, k, :], xt_l[:, par, k, :], k == 0, k == KD - 1)
                    sig(last, h1_ps)
                    need(pe, prod_ready, *((n, j - 1) if j >= 2 else (n - 1, FB - 1 + j)))
                    for k in range(KD):
                        cols = slice(k * P, (k + 1) * P)
                        last = product(nc, bank[4 + b][:, :], w3_h[:, j, cols], w3_l[:, j, cols],
                                       xt_h[:, par, k, :], xt_l[:, par, k, :], k == 0, k == KD - 1)
                    sig(last, h3_ps)
                elif kind == "D":
                    need(pe, gh_ready, n, j + 1)
                    need(pe, gl_ready, n, j + 1)
                    if j == 0:
                        need(pe, ob_ready, n - 1, 2)
                    for c in range(CH):
                        tok = slice(c * P, (c + 1) * P)
                        at = (c % 2) * DM
                        last = product(nc, bank[c // 2][:, at:at + DM], g_h[:, j % 2, tok], g_l[:, j % 2, tok],
                                       w2_h[:, j, :], w2_l[:, j, :], j == 0 and c % 2 == 0,
                                       j == FB - 1 and c % 2 == 1)
                    sig(last, down_ps)
                elif kind == "G":
                    need(pe, lg_ready, n, 1)
                    need_alone(pe, xtl_ready, n, KD, carrier)
                    for c in range(CH):
                        last = nc.tensor.transpose(bank[6][:, c * 32:(c + 1) * 32],
                                                   lg[GROW:P, c * P:(c + 1) * P], ident[GROW:P, GROW:P])
                    sig(last, lg_ps)
                elif kind == "C":
                    need(pe, route, n, R_ALL)
                    for c in range(CH):
                        last = nc.tensor.transpose(bank[7][0:2 * E, c * P:(c + 1) * P],
                                                   cw_parts[:, c, :], ident[:, :])
                    sig(last, cwt_ps)
                elif kind == "S":
                    need(pe, cwt_ready, n, 1)
                    need(pe, lgt_ready, n, 1)
                    sig(nc.tensor.matmul(bank[6][:, :], sel[:, :], cwt[:, :], start=True, stop=True), cwb_ps)
                elif kind == "X":
                    need(pe, cwb_ready, n, 1)
                    transposes(n + 1, 1 - par)

            pe.wait_ge(consts.handle, 1)
            transposes(0, 0)
            run(pe, piece)

        @block.scalar
        def _(act):
            A = nc.scalar.activation

            def split_xt(n, par):
                for k in range(KD):
                    need(act, xt_ps, n, k + 1)
                    sig(A(xt_h[:, par, k, :], bank[6 + k][:, :], ACT.Copy), xth_ready)

            def split_weights(b):
                act.wait_ge(w_in[group_of[b]].handle, 48)
                for dst, src in ((w1_h, w1_f), (w3_h, w3_f), (w2_h, w2_f)):
                    sig(A(dst[:, b, :], src[:, b, :], ACT.Copy), wh_ready)

            def piece(kind, j, n, par, loads, first):
                if kind == "F":
                    need(act, h1_ps, n, j + 1)
                    need(act, prod_ready, *((n, j - 1) if j >= 2 else (n - 1, FB - 1 + j)))
                    sig(A(act1[:, j % 2, :], bank[2 + j % 2][:, :], ACT.Silu), act_ready)
                    if j == 0:
                        sig(A(lg[GROW:P, :], bank[2][GROW:P, :], ACT.Copy), lg_ready)
                    if first and j + 2 < FB:
                        split_weights(j + 2)
                elif kind == "H":
                    if j < SB:
                        need(act, prod_ready, n, j + 1)
                    else:
                        need(act, g_ready, n, j - SB + 1)
                    need(act, down_ps, *((n, j - 1) if j >= 2 else (n - 1, FB - 1 + j)))
                    sig(A(g_h[:, j % 2, :], g[:, j % 2, :], ACT.Copy), gh_ready)
                elif kind == "G":
                    need(act, lg_ps, n, 1)
                    sig(A(lgt[:, :, :], bank[6][:, 0:CH * 32].rearrange("p (c e) -> p c e", c=CH)[:, :, 0:E],
                          ACT.Copy), lgt_ready)
                    need(act, route, n, R_SHIFT)
                    sig(A(ep[:, :, :], shifted[:, :, :], ACT.Exp), ep_ready)
                elif kind == "C":
                    need(act, cwt_ps, n, 1)
                    sig(A(cwt[:, :], bank[7][0:2 * E, :], ACT.Copy), cwt_ready)
                elif kind == "S":
                    need(act, cwb_ps, n, 1)
                    sig(A(cwb[:, :], bank[6][:, :], ACT.Copy), cwb_ready)
                elif kind == "X":
                    split_xt(n + 1, 1 - par)

            split_weights(0)
            split_xt(0, 0)
            split_weights(1)
            run(act, piece)

        @block.vector
        def _(dve):
            V = nc.vector

            def statistics(n, par, loads):
                dve.wait_ge(x1_loaded[par].handle, 16 * loads)
                for c in range(CH):
                    sig(V.bn_stats(bst[:, c, :], x1[par][:, c, :]), stats_ready)
                for c in range(CH):
                    need_alone(dve, stats_ready, n, c + 1, carrier)
                    sig(V.bn_aggr(mv[:, c, :], bst[:, c, :]), mv_ready)

            def normalise(n, par):
                need(dve, rstd_ready, n, 1)
                need(dve, xt_ps, n - 1, KD)
                for c in range(CH):
                    sig(V.tensor_scalar(xn[:, c, :], x1[par][:, c, :], mv[:, c, 0:1], rstd[:, c:c + 1],
                                        ALU.subtract, ALU.mult), xn_ready)

            def split_xt(n, par):
                for k in range(KD):
                    need(dve, xth_ready, n, k + 1)
                    sig(V.tensor_tensor(xt_l[:, par, k, :], bank[6 + k][:, :],
                                        xt_h[:, par, k, :].bitcast(F32), ALU.subtract), xtl_ready)

            def split_weights(b):
                for m, (dst, src, hi) in enumerate(((w1_l, w1_f, w1_h), (w3_l, w3_f, w3_h),
                                                    (w2_l, w2_f, w2_h))):
                    dve.wait_ge(wh_ready.handle, 3 * b + m + 1)
                    sig(V.tensor_tensor(dst[:, b, :], src[:, b, :], hi[:, b, :].bitcast(F32),
                                        ALU.subtract), wl_ready)

            def routing(n, part):
                per_tok = lambda ap: ap.unsqueeze(2).to_broadcast([P, CH, E])
                ranks = rank[:, :].unsqueeze(1).to_broadcast([P, CH, E])
                done = [0 if part == 0 else R_PART]

                def link(ins):
                    sig(ins, route)
                    done[0] += 1
                    need(dve, route, n, done[0])

                def best(left, pick):
                    link(V.tensor_reduce(top[:, :], left[:, :, :], AX.X, ALU.max))
                    link(V.tensor_tensor(tied[:, :, :], left[:, :, :], per_tok(top[:, :]), ALU.is_equal))
                    link(V.tensor_tensor(tied_rank[:, :, :], tied[:, :, :], ranks, ALU.mult))
                    link(V.tensor_reduce(best_rank[:, :], tied_rank[:, :, :], AX.X, ALU.max))
                    link(V.tensor_tensor(pick[:, :, :], tied_rank[:, :, :], per_tok(best_rank[:, :]),
                                         ALU.is_equal))

                if part == 0:
                    need(dve, lgt_ready, n, 1)
                    link(V.tensor_reduce(top[:, :], lgt[:, :, :], AX.X, ALU.max))
                    link(V.tensor_tensor(shifted[:, :, :], lgt[:, :, :], per_tok(top[:, :]), ALU.subtract))
                    assert done[0] == R_SHIFT
                    need(dve, ep_ready, n, 1)
                    link(V.tensor_reduce(total[:, :], ep[:, :, :], AX.X, ALU.add))
                    link(V.reciprocal(inv[:, :], total[:, :]))
                    link(V.tensor_tensor(score[:, :, :], ep[:, :, :], per_tok(inv[:, :]), ALU.mult))
                    assert done[0] == R_PART
                else:
                    best(score, pick1)
                    link(V.scalar_tensor_tensor(rest[:, :, :], pick1[:, :, :], -2.0, score[:, :, :],
                                                ALU.mult, ALU.add))
                    best(rest, pick2)
                    link(V.tensor_tensor(tied[:, :, :], pick1[:, :, :], pick2[:, :, :], ALU.add))
                    link(V.tensor_tensor(cw[:, :, :], score[:, :, :], tied[:, :, :], ALU.mult))
                    link(V.tensor_copy(cw_r[:, :, :], cw[:, :, :]))
                    link(V.tensor_copy(cw_parts[:, :, 0:E], cw_r[:, :, :].bitcast(F32)))
                    link(V.tensor_tensor(cw_parts[:, :, E:2 * E], cw[:, :, :], cw_r[:, :, :].bitcast(F32),
                                         ALU.subtract))
                    assert done[0] == R_ALL

            def piece(kind, j, n, par, loads, first):
                if kind == "F":
                    need(dve, act_ready, n, j + 1)
                    need(dve, h3_ps, n, j + 1)
                    need(dve, gl_ready, *((n, j - 1) if j >= 2 else (n - 1, FB - 1 + j)))
                    sig(V.tensor_tensor(g[:, j % 2, :], bank[4 + j % 2][:, :], act1[:, j % 2, :], ALU.mult),
                        prod_ready)
                    if first and j + 2 < FB:
                        split_weights(j + 2)
                elif kind in "GR":
                    routing(n, 0 if kind == "G" else 1)
                elif kind == "H" and j >= SB:
                    if j == SB:
                        need(dve, cwb_ready, n, 1)
                    need(dve, prod_ready, n, j + 1)
                    sig(V.tensor_tensor(g[:, j % 2, :], g[:, j % 2, :], cwb[:, :], ALU.mult), g_ready)
                elif kind == "K":
                    need(dve, stored, n - 1, 16)
                    need(dve, down_ps, n, FB)
                    for t in range(2):
                        sig(V.tensor_tensor(flat(ob[:, 2 * t:2 * t + 2, :]), bank[t][:, :],
                                            flat(x1[par][:, 2 * t:2 * t + 2, :]), ALU.add), ob_ready)
                elif kind == "L":
                    statistics(n + 1, 1 - par, loads)
                elif kind == "N":
                    normalise(n + 1, 1 - par)
                elif kind == "X":
                    split_xt(n + 1, 1 - par)

            statistics(0, 0, 1)
            normalise(0, 0)
            split_weights(0)
            split_xt(0, 0)
            split_weights(1)
            run(dve, piece)

        @block.gpsimd
        def _(pool):
            G = nc.gpsimd

            def rstd_of(n):
                need_alone(pool, mv_ready, n, CH, carrier)
                sig(G.tensor_scalar(ve[:, :], mv[:, :, 1], EPS, None, ALU.add), ve_ready)
                need(pool, ve_ready, n, 1)
                sig(G.tensor_tensor(rstd[:, :], ve[:, :], neg_half[:, :], ALU.pow), rstd_ready)

            def piece(kind, j, n, par, loads, first):
                if kind == "H":
                    need(pool, gh_ready, n, j + 1)
                    sig(G.tensor_tensor(g_l[:, j % 2, :], g[:, j % 2, :], g_h[:, j % 2, :].bitcast(F32),
                                        ALU.subtract), gl_ready)
                elif kind == "L":
                    rstd_of(n + 1)

            const = [0]

            def made(ins):
                ins.then_inc(const_step.handle, 1)
                const[0] += 1

            made(G.memset(ident[:, :], 0.0))
            made(G.memset(neg_half[:, :], -0.5))
            made(G.memset(sel_f[:, :, :], 1.0))
            for e in range(E):
                made(G.memset(rank[:, e:e + 1], float(E - e)))
            pool.wait_ge(const_step.handle, const[0])
            made(G.affine_select(out=ident[:, :], in_=ident[:, :], compare_op=ALU.not_equal, fill=1.0,
                                 base=0, pattern=[[-1, P]], channel_multiplier=1))
            wide = P // E
            for k in range(2):
                made(G.affine_select(out=sel_f[:, k, :], in_=sel_f[:, k, :], compare_op=ALU.is_ge, fill=0.0,
                                     base=k * P, pattern=[[1, P]], channel_multiplier=-wide))
            pool.wait_ge(const_step.handle, const[0])
            for k in range(2):
                made(G.affine_select(out=sel_f[:, k, :], in_=sel_f[:, k, :], compare_op=ALU.is_ge, fill=0.0,
                                     base=wide - 1 - k * P, pattern=[[-1, P]], channel_multiplier=wide))
            pool.wait_ge(const_step.handle, const[0])
            G.tensor_tensor(sel[:, :], sel_f[:, 0, :], sel_f[:, 1, :], ALU.add).then_inc(consts.handle, 1)
            rstd_of(0)
            run(pool, piece)


def build(nc, u, win, wo, vec, w1, w3, w2, out):
    NS = u.shape[0] * u.shape[1] // TOK
    u_v = u.rearrange("b (n c p) d -> (b n) p c d", c=CH, p=P)
    out_v = out.rearrange("b (n c p) d -> (b n) p c d", c=CH, p=P)
    x1_d = nc.dram_tensor("x1_between_phases", (NS, P, CH, DM), F32).ap()
    with ExitStack() as ctx:
        x1_first = ctx.enter_context(nc.sbuf_tensor("x1_first", [P, CH, DM], F32))[:, :, :]
        x1_loaded, x1_stored = ([Count(ctx.enter_context(nc.semaphore(f"{name}{k}")), 1, False)
                                 for k in range(2)] for name in ("x1_loaded", "x1_stored"))
        mixer(nc, NS, u_v, win, wo, vec, x1_d, x1_first, x1_loaded, x1_stored)
        experts(nc, NS, x1_d, x1_first, x1_loaded, x1_stored, w1, w3, w2, out_v)


def kernel(**inputs):
    import numpy as np
    import concourse.bacc as bacc
    from concourse.bass_utils import run_bass_kernel_spmd

    x = {k: np.asarray(v) for k, v in inputs.items()}
    f32 = np.float32
    u = np.ascontiguousarray(x["L0_attn_u"])

    w = x["L0_attn_in_proj_w"].T
    w = np.concatenate([w[:, DI + XBC:], w[:, :DI], w[:, DI:DI + XBC]], axis=1)
    win = np.ascontiguousarray(w.reshape(KD, P, WIN).transpose(1, 0, 2))
    wo = np.ascontiguousarray(x["L0_attn_out_proj_w"].T.reshape(KI, P, DM).transpose(1, 0, 2))

    vec = np.zeros((P, V_ALL), f32)
    vec[:, V_TAP:V_BIAS] = x["L0_attn_conv_w"].reshape(NB, P, TAPS).transpose(1, 0, 2).reshape(P, -1)
    vec[:, V_BIAS:V_NORM] = x["L0_attn_conv_b"].reshape(NB, P).T
    vec[:, V_NORM:V_DT] = x["L0_attn_norm_w"].reshape(KI, P).T
    vec[:, V_DT:V_A] = x["L0_attn_dt_bias"]
    vec[:, V_A:V_D] = x["L0_attn_A_log"]
    vec[:, V_D:] = x["L0_attn_D"]

    def up(shared, routed, gate=None):
        cols = np.zeros((DM, FB, P), f32)
        cols[:, 0, :GROW] = shared[:, (SB - 1) * P:]
        cols[:, 1:SB] = shared[:, :(SB - 1) * P].reshape(DM, SB - 1, P)
        if gate is not None:
            cols[:, 0, GROW:GROW + E] = gate
        cols[:, SB:] = routed.transpose(1, 0, 2).reshape(DM, E, RB, FE // RB).transpose(0, 2, 1, 3)\
            .reshape(DM, RB, P)
        return np.ascontiguousarray(cols.reshape(KD, P, FB, P).transpose(1, 2, 0, 3).reshape(P, FB, KD * P))

    w1 = up(x["L0_ffn_sw1"], x["L0_ffn_rw1"], x["L0_ffn_gate_w"])
    w3 = up(x["L0_ffn_sw3"], x["L0_ffn_rw3"])
    w2 = np.zeros((P, FB, DM), f32)
    s2, r2 = x["L0_ffn_sw2"], x["L0_ffn_rw2"]
    w2[:GROW, 0] = s2[(SB - 1) * P:]
    w2[:, 1:SB] = s2[:(SB - 1) * P].reshape(SB - 1, P, DM).transpose(1, 0, 2)
    w2[:, SB:] = r2.reshape(E, RB, FE // RB, DM).transpose(0, 2, 1, 3).reshape(P, RB, DM)

    nc = bacc.Bacc("TRN2", target_bir_lowering=False, num_devices=1)
    arrays = dict(u_in=u, win_in=win, wo_in=wo, vec_in=vec, w1_in=w1, w3_in=w3, w2_in=w2)
    args = [nc.dram_tensor(name, a.shape, mybir.dt.from_np(a.dtype), kind="ExternalInput").ap()
            for name, a in arrays.items()]
    out = nc.dram_tensor("out", u.shape, F32, kind="ExternalOutput").ap()
    build(nc, *args, out)
    result = run_bass_kernel_spmd(nc, [arrays], core_ids=[0])
    return result.results[0]["out"]
```
